# Optimizing a Trainium2 kernel written in Bass

```python
import numpy as np
import jax
import jax.numpy as jnp

def _softmax(x, axis=-1):
    return jax.nn.softmax(x, axis=axis)

def _gelu(x):
    return jax.nn.gelu(x, approximate=True)

def _silu(x):
    return jax.nn.silu(x)

def _sigmoid(x):
    return jax.nn.sigmoid(x)

def _layernorm(x, axis=-1, eps=1e-05):
    m = jnp.mean(x, axis=axis, keepdims=True)
    v = jnp.var(x, axis=axis, keepdims=True)
    return (x - m) / jnp.sqrt(v + eps)

def _scatter_add(tgt, idx, src, axis=0):
    return tgt.at[idx].add(src)

def _segment_sum(src, seg, n):
    return jax.ops.segment_sum(src, seg, n)
kernel_name = 'mk_recurrent_d1_jaxref_r4_1ab953'

def setup_inputs(seed: int=0):
    np.random.seed(seed)
    _w = jnp.asarray

    def _L0_attn_setup():
        import jax, jax.numpy as jnp
        import numpy as np
        D_MODEL = 256
        NUM_HEADS = 16
        HEAD_DIM = D_MODEL // NUM_HEADS
        SCALE = float(np.sqrt(HEAD_DIM))

        def _xavier(key, shape):
            fan_out, fan_in = shape
            lim = float(np.sqrt(6.0 / (fan_in + fan_out)))
            return jax.random.uniform(key, shape, jnp.float32, -lim, lim)
        key = jax.random.key(seed)
        kx, kqkv, ko = jax.random.split(key, 3)
        B, T = (2, 512)
        x = jax.random.normal(kx, (B, T, D_MODEL), jnp.float32)
        W_qkv = _xavier(kqkv, (3 * D_MODEL, D_MODEL))
        b_qkv = jnp.zeros((3 * D_MODEL,), jnp.float32)
        W_o = _xavier(ko, (D_MODEL, D_MODEL))
        b_o = jnp.zeros((D_MODEL,), jnp.float32)
        return {'x': x, 'W_qkv': W_qkv, 'b_qkv': b_qkv, 'W_o': W_o, 'b_o': b_o}
    _L0_attn_in = _L0_attn_setup()

    def _L0_ffn_setup():
        import jax, jax.numpy as jnp
        import numpy as np
        E = 16
        K = 4
        NG = 4
        TG = 2
        SCALE = 2.5
        NORM_TOPK = True
        H = 256
        I = 128
        SH_I = I * 2
        B, S = (2, 512)
        key = jax.random.key(seed)
        ks = jax.random.split(key, 9)

        def w(k, shape, fan_in):
            return jax.random.normal(k, shape, jnp.float32) * (1.0 / np.sqrt(fan_in))
        return {'hidden_states': jax.random.normal(ks[0], (B, S, H), jnp.float32), 'gate_w': w(ks[1], (E, H), H), 'gate_bias': jnp.zeros((E,), jnp.float32), 'Wg': w(ks[2], (E, I, H), H), 'Wu': w(ks[3], (E, I, H), H), 'Wd': w(ks[4], (E, H, I), I), 'Ws_g': w(ks[5], (SH_I, H), H), 'Ws_u': w(ks[6], (SH_I, H), H), 'Ws_d': w(ks[7], (H, SH_I), SH_I)}
    _L0_ffn_in = _L0_ffn_setup()
    _d = {'L0_attn_x': _L0_attn_in['x'], 'L0_attn_W_qkv': _L0_attn_in['W_qkv'], 'L0_attn_b_qkv': _L0_attn_in['b_qkv'], 'L0_attn_W_o': _L0_attn_in['W_o'], 'L0_attn_b_o': _L0_attn_in['b_o'], 'L0_ffn_gate_w': _L0_ffn_in['gate_w'], 'L0_ffn_gate_bias': _L0_ffn_in['gate_bias'], 'L0_ffn_Wg': _L0_ffn_in['Wg'], 'L0_ffn_Wu': _L0_ffn_in['Wu'], 'L0_ffn_Wd': _L0_ffn_in['Wd'], 'L0_ffn_Ws_g': _L0_ffn_in['Ws_g'], 'L0_ffn_Ws_u': _L0_ffn_in['Ws_u'], 'L0_ffn_Ws_d': _L0_ffn_in['Ws_d']}
    _x0 = _d['L0_attn_x']
    _d['L0_attn_x'] = jax.random.normal(jax.random.fold_in(jax.random.key(seed), 1), (4, 1024, 256), dtype=_x0.dtype)
    del _x0
    return _d

def reference(L0_attn_x, L0_attn_W_qkv, L0_attn_b_qkv, L0_attn_W_o, L0_attn_b_o, L0_ffn_gate_w, L0_ffn_gate_bias, L0_ffn_Wg, L0_ffn_Wu, L0_ffn_Wd, L0_ffn_Ws_g, L0_ffn_Ws_u, L0_ffn_Ws_d):

    def _L0_attn_ref(x, W_qkv, b_qkv, W_o, b_o):
        import jax, jax.numpy as jnp
        import numpy as np
        D_MODEL = 256
        NUM_HEADS = 16
        HEAD_DIM = D_MODEL // NUM_HEADS
        SCALE = float(np.sqrt(HEAD_DIM))

        def _xavier(key, shape):
            fan_out, fan_in = shape
            lim = float(np.sqrt(6.0 / (fan_in + fan_out)))
            return jax.random.uniform(key, shape, jnp.float32, -lim, lim)
        B, T, C = x.shape
        qkv = x @ W_qkv.T + b_qkv
        qkv = qkv.reshape(B, T, 3, NUM_HEADS, HEAD_DIM)
        qkv = jnp.transpose(qkv, (2, 0, 3, 1, 4))
        Q, K, V = (qkv[0], qkv[1], qkv[2])
        scores = jnp.einsum('bhqd,bhkd->bhqk', Q, K) / SCALE
        attn = jax.nn.softmax(scores, axis=-1)
        out = jnp.einsum('bhqk,bhkd->bhqd', attn, V)
        out = jnp.transpose(out, (0, 2, 1, 3)).reshape(B, T, C)
        return out @ W_o.T + b_o

    def _L0_ffn_ref(hidden_states, gate_w, gate_bias, Wg, Wu, Wd, Ws_g, Ws_u, Ws_d):
        import jax, jax.numpy as jnp
        import numpy as np
        E = 16
        K = 4
        NG = 4
        TG = 2
        SCALE = 2.5
        NORM_TOPK = True
        H = 256
        I = 128
        SH_I = I * 2
        B, S = (2, 512)
        x = hidden_states
        b, s, h = x.shape
        n = b * s
        xf = x.reshape(n, h)
        logits = xf @ gate_w.T
        scores = jax.nn.sigmoid(logits)
        sfc = scores + gate_bias
        epg = E // NG
        grp = sfc.reshape(n, NG, epg)
        g_scores = jax.lax.top_k(grp, 2)[0].sum(-1)
        _, gidx = jax.lax.top_k(g_scores, TG)
        gmask = jax.nn.one_hot(gidx, NG, dtype=sfc.dtype).sum(1)
        emask = jnp.repeat(gmask, epg, axis=1)
        masked = jnp.where(emask > 0, sfc, -jnp.inf)
        _, topk_idx = jax.lax.top_k(masked, K)
        topk_w = jnp.take_along_axis(scores, topk_idx, axis=1)
        if K > 1 and NORM_TOPK:
            topk_w = topk_w / (topk_w.sum(-1, keepdims=True) + 1e-20)
        topk_w = topk_w * SCALE
        cw = (jax.nn.one_hot(topk_idx, E, dtype=topk_w.dtype) * topk_w[..., None]).sum(1)
        hg = jnp.einsum('nh,eih->nei', xf, Wg)
        hu = jnp.einsum('nh,eih->nei', xf, Wu)
        act = jax.nn.silu(hg) * hu
        y = jnp.einsum('nei,ne,ehi->nh', act, cw, Wd)
        shared = jax.nn.silu(xf @ Ws_g.T) * (xf @ Ws_u.T) @ Ws_d.T
        y = y + shared
        return (x + y.reshape(b, s, h)).astype(hidden_states.dtype)
    x = L0_attn_x
    xn = _layernorm(x, axis=-1)
    s = _L0_attn_ref(xn, L0_attn_W_qkv, L0_attn_b_qkv, L0_attn_W_o, L0_attn_b_o)
    g = _silu(_L0_ffn_ref(xn, L0_ffn_gate_w, L0_ffn_gate_bias, L0_ffn_Wg, L0_ffn_Wu, L0_ffn_Wd, L0_ffn_Ws_g, L0_ffn_Ws_u, L0_ffn_Ws_d))
    x = x + s * g
    return x

_drawn_inputs = setup_inputs


def setup_inputs(seed=0):
    import zlib

    import numpy as np

    out = dict(_drawn_inputs(seed))
    spreads = {'L0_attn_b_qkv': (0.0, 0.1), 'L0_attn_b_o': (0.0, 0.1), 'L0_ffn_gate_bias': (0.0, 0.1)}
    factors = {}
    for name, (base, spread) in spreads.items():
        noise = np.random.default_rng([zlib.crc32(name.encode()), seed]).standard_normal(out[name].shape)
        drawn = base * np.exp(spread * noise) if base else spread * noise
        out[name] = jnp.asarray(drawn.astype(out[name].dtype))
    for name, factor in factors.items():
        out[name] = (out[name] * factor).astype(out[name].dtype)
    return out
```

```python
from contextlib import ExitStack

import concourse.bass as bass
from concourse import mybir

F32 = mybir.dt.float32
BF16 = mybir.dt.bfloat16
ALU = mybir.AluOpType
ACT = mybir.ActivationFunctionType
AX = mybir.AxisListType

P = 128
NB, T, D = 4, 1024, 256
HEADS, HD = 16, 16
N = NB * T
TILES = N // P
TB = T // P
KC = D // P
E, TOPK, NG, TG = 16, 4, 4, 2
EPG = E // NG
I = 128
NE = E + 2
CH = 512
CT = CH // P
CPB = T // CH
HPG = 4
GROUPS = NB * HEADS // HPG
GPB = HEADS // HPG
VW = HD + 1
KT = T // P
PARTS = 3
STACK = 6 * HD
ROWS = STACK + PARTS
EPS = 1e-5
ROUTE_SCALE = 2.5
PRODUCTS = [(0, 0), (1, 0), (2, 0), (0, 1), (1, 1), (0, 2)]


def ds(start, size):
    return bass.ds(start, size)


class Link:

    def __init__(self, eng, sem, start=0):
        self.eng, self.sem, self.start, self.n = eng, sem, start, 0

    def put(self, ins):
        ins.then_inc(self.sem, 1)
        self.n += 1

    def wait(self):
        self.eng.wait_ge(self.sem, self.start + self.n)

    def __call__(self, ins):
        self.put(ins)
        self.wait()


def project_and_ffn(nc, t, scr, xg, ident):
    with ExitStack() as ctx:
        sb = lambda name, shape, dt=F32: ctx.enter_context(nc.sbuf_tensor(name, shape, dt))
        sem = lambda name: ctx.enter_context(nc.semaphore(name))
        wqk = sb("wqk_sb", [P, KC, 2 * D])
        wvg = sb("wvg_sb", [P, KC, D + E])
        bqk = sb("bqk_sb", [P, 4])
        bv = sb("bv_sb", [P, D])
        gbias = sb("gbias_sb", [P, E])
        wg = sb("wg_sb", [P, KC, NE * I])
        wu = sb("wu_sb", [P, KC, NE * I])
        wd = sb("wd_sb", [P, NE, D])
        stats = sb("stats", [P, TB, 6])
        ln = sb("ln", [P, 8, TB])
        xnb = sb("xnb", [P, TB, D])
        xT = sb("xT", [P, KC, T])
        qk32 = sb("qk32", [P, 2, CH])
        rest = sb("rest", [P, 2, CH])
        parts = sb("parts", [P, 2, PARTS, CH], BF16)
        vst = sb("vst", [P, GPB, KT, HPG, VW])
        logit = sb("logit", [P, TB, E])
        score = sb("score", [P, TB, E])
        sfc = sb("sfc", [P, TB, E])
        beats = sb("beats", [P, TB, E])
        rank = sb("rank", [P, TB, E])
        cw = sb("cw", [P, TB, E])
        top = sb("top", [P, 8, TB, NG])
        wsum = sb("wsum", [P, TB])
        sg = sb("sg", [P, 2, CH])
        act = sb("act", [P, 2, CH])
        yacc = sb("yacc", [P, CT, D])
        gu = ctx.enter_context(nc.psum_tensor("gu", [P, 4, 512], F32))
        yy = ctx.enter_context(nc.psum_tensor("yy", [P, 4, 512], F32))

        x_first, x_rest, w_in, wffn_in = sem("x_first"), sem("x_rest"), sem("w_in"), sem("wffn_in")
        ident_zero, ident_ready = sem("ident_zero"), sem("ident_ready")
        dve_link = sem("dve_link")
        var_ready, std_ready, xn_ready = sem("var_ready"), sem("std_ready"), sem("xn_ready")
        xnb_ready = sem("xnb_ready")
        t_done = sem("t_done")
        xT_act, xT_dve = sem("xT_act"), sem("xT_dve")
        v_ready, v_copied = sem("v_ready"), sem("v_copied")
        v_stored = sem("v_stored")
        qk_ready, qk_copied = sem("qk_ready"), sem("qk_copied")
        rest_ready, mid_ready, split_done = sem("rest_ready"), sem("mid_ready"), sem("split_done")
        parts_stored = [sem(f"parts_stored{i}") for i in range(2)]
        sig_ready, cw_ready = sem("sig_ready"), sem("cw_ready")
        g_ready, u_ready = sem("g_ready"), sem("u_ready")
        silu_done, act_done = sem("silu_done"), sem("act_done")
        y_ready, y_added = sem("y_ready"), sem("y_added")
        g_done = sem("g_done")
        block = ctx.enter_context(nc.Block())

        @block.sync
        def _(sp):
            xv = t["x"].rearrange("(t p) d -> p t d", p=P)
            sp.dma_start(xg[:, 0:TB, :], xv[:, 0:TB, :]).then_inc(x_first, 16)
            sp.dma_start(wvg[:], t["wvg"]).then_inc(w_in, 16)
            sp.dma_start(wqk[:], t["wqk"]).then_inc(w_in, 16)
            sp.dma_start(bqk[:], t["bqk"]).then_inc(w_in, 16)
            sp.dma_start(bv[:], t["bv"].to_broadcast([P, D])).then_inc(w_in, 16)
            sp.dma_start(gbias[:], t["gbias"].to_broadcast([P, E])).then_inc(w_in, 16)
            for b in range(1, NB):
                sp.dma_start(xg[:, b * TB:(b + 1) * TB, :], xv[:, b * TB:(b + 1) * TB, :]).then_inc(x_rest, 16)
            sp.dma_start(wg[:], t["wg"]).then_inc(wffn_in, 16)
            sp.dma_start(wu[:], t["wu"]).then_inc(wffn_in, 16)
            sp.dma_start(wd[:], t["wd"]).then_inc(wffn_in, 16)
            sp.sem_inc(v_stored, 16)
            for s in parts_stored:
                sp.sem_inc(s, 32)
            with sp.Fori(0, NB) as b:
                sp.wait_ge(v_copied, TB * b + TB + 2)
                sp.dma_start(scr["v"][ds(b * GPB, GPB)].rearrange("g p n -> p g n"),
                             vst[:].rearrange("p g k j w -> p g (k j w)")).then_inc(v_stored, 16)
                for n in range(2 * 4):
                    half, m = n // 4, n % 4
                    sp.wait_ge(split_done, 8 * b + n + 1)
                    for i in range(2):
                        group = 4 * b + (m % 2) * 2 + i
                        sp.dma_start(
                            scr["qk"][ds(group, 1), m // 2].rearrange("a s r t -> r (a s) t")[
                                :, :, half * CH:(half + 1) * CH],
                            parts[64 * i:64 * i + 64, n % 2],
                        ).then_inc(parts_stored[n % 2], 16)
            sp.wait_ge(v_stored, 16 + 16 * NB)
            for s in parts_stored:
                sp.wait_ge(s, 32 + 4 * 32 * NB)

        @block.gpsimd
        def _(pool):
            nc.gpsimd.memset(ident[:], 0.0).then_inc(ident_zero, 1)
            pool.wait_ge(ident_zero, 1)
            nc.gpsimd.affine_select(out=ident[:], in_=ident[:], compare_op=ALU.not_equal, fill=1.0, base=0,
                                    pattern=[[-1, P]], channel_multiplier=1).then_inc(ident_ready, 1)
            with pool.Fori(0, NB) as b:
                for n in range(2 * 4):
                    k = 8 * b + n
                    pool.wait_ge(qk_copied, k + 1 + 4)
                    nc.gpsimd.tensor_tensor(rest[:, n % 2], qk32[:, n % 2], parts[:, n % 2, 0], ALU.subtract)\
                        .then_inc(rest_ready, 1)
                    pool.wait_ge(mid_ready, k + 1)
                    nc.gpsimd.tensor_tensor(parts[:, n % 2, 2], rest[:, n % 2], parts[:, n % 2, 1], ALU.subtract)\
                        .then_inc(split_done, 1)

        @block.scalar
        def _(a):
            a.sem_inc(qk_copied, 4)
            a.sem_inc(silu_done, 2)
            a.sem_inc(g_done, 1)
            with a.Fori(0, NB) as b:
                a.wait_ge(var_ready, b + 1)
                nc.scalar.activation(ln[:, 4], ln[:, 3], ACT.Sqrt).then_inc(std_ready, 1)
            a.wait_ge(w_in, 80)
            with a.Fori(0, NB) as b:
                a.wait_ge(xn_ready, b + 1)
                a.wait_ge(t_done, 2 * b + 1)
                nc.scalar.copy(xnb[:], xg[:, ds(b * TB, TB), :]).then_inc(xnb_ready, 1)
                for half in range(CPB):
                    a.wait_ge(t_done, 2 * b + half + 2)
                    nc.scalar.copy(xT[:, 0, half * CH:(half + 1) * CH], yy[:, 0, :]).then_inc(xT_act, 1)
                a.wait_ge(v_copied, TB * b + TB + 2)
                nc.scalar.activation(score[:], logit[:], ACT.Sigmoid).then_inc(sig_ready, 1)
                for n in range(2 * 4 + 1):
                    k = 8 * b + n
                    if n < 8:
                        a.wait_ge(qk_ready, k + 1)
                        a.wait_ge(parts_stored[n % 2], 32 * (4 * b + n // 2 + 1))
                        nc.scalar.activation(qk32[:, n % 2], gu[:, n % 4], ACT.Identity,
                                             bias=bqk[:, n % 4:n % 4 + 1])
                        nc.scalar.activation(parts[:, n % 2, 0], gu[:, n % 4], ACT.Identity,
                                             bias=bqk[:, n % 4:n % 4 + 1]).then_inc(qk_copied, 1)
                    if n > 0:
                        a.wait_ge(rest_ready, k)
                        nc.scalar.copy(parts[:, (n - 1) % 2, 1], rest[:, (n - 1) % 2]).then_inc(mid_ready, 1)
                with a.Fori(0, CPB) as c:
                    for e in range(NE):
                        n = b * (CPB * NE) + c * NE + e
                        a.wait_ge(g_ready, n + 1)
                        a.wait_ge(act_done, n + 1)
                        nc.scalar.activation(sg[:, e % 2], gu[:, e % 2], ACT.Silu).then_inc(silu_done, 1)
                    a.wait_ge(y_added, b * (CPB * NE) + c * NE + NE + 2)
                    nc.scalar.activation(xg[:, ds(b * TB + c * CT, CT), :], yacc[:], ACT.Silu).then_inc(g_done, 1)

        @block.vector
        def _(v):
            nc.vector.memset(vst[:], 1.0)
            v.sem_inc(v_copied, 2)
            v.sem_inc(act_done, 2)
            v.sem_inc(y_added, 2)

            LN_LINKS = 12

            def layernorm(b):
                link = Link(v, dve_link, b * LN_LINKS)
                for k in range(TB):
                    ins = nc.vector.bn_stats(stats[:, k, :], xg[:, b * TB + k, :])
                link(ins)
                even, odd = stats[:, :, 0:3], stats[:, :, 3:6]
                link.put(nc.vector.tensor_tensor(ln[:, 0], even[:, :, 1], odd[:, :, 1], ALU.add))
                link.put(nc.vector.tensor_tensor(ln[:, 1], even[:, :, 1], odd[:, :, 1], ALU.subtract))
                link(nc.vector.tensor_tensor(ln[:, 2], even[:, :, 2], odd[:, :, 2], ALU.add))
                link.put(nc.vector.scalar_tensor_tensor(ln[:, 5], ln[:, 1], 0.25, ln[:, 1], ALU.mult, ALU.mult))
                link.put(nc.vector.tensor_scalar(ln[:, 6], ln[:, 2], 1.0 / D, EPS, ALU.mult, ALU.add))
                link(nc.vector.tensor_scalar(ln[:, 0], ln[:, 0], 0.5, None, ALU.mult))
                nc.vector.tensor_tensor(ln[:, 3], ln[:, 5], ln[:, 6], ALU.add).then_inc(var_ready, 1)
                v.wait_ge(std_ready, b + 1)
                link(nc.vector.reciprocal(ln[:, 5], ln[:, 4]))
                link(nc.vector.tensor_tensor(ln[:, 6], ln[:, 5], ln[:, 5], ALU.mult))
                link(nc.vector.tensor_tensor(ln[:, 6], ln[:, 6], ln[:, 3], ALU.mult))
                link(nc.vector.tensor_scalar(ln[:, 6], ln[:, 6], -0.5, 1.5, ALU.mult, ALU.add))
                link(nc.vector.tensor_tensor(ln[:, 7], ln[:, 5], ln[:, 6], ALU.mult))
                for k in range(TB):
                    row = xg[:, ds(b * TB + k, 1), :].rearrange("p a d -> p (a d)")
                    ins = nc.vector.tensor_scalar(row, row, ln[:, 0, k:k + 1], ln[:, 7, k:k + 1],
                                                  ALU.subtract, ALU.mult)
                ins.then_inc(xn_ready, 1)
                v.wait_ge(xn_ready, b + 1)
                assert link.n == LN_LINKS, link.n

            v.wait_ge(x_first, 16)
            layernorm(0)
            v.wait_ge(x_rest, 16 * (NB - 1))
            with v.Fori(1, NB) as b:
                layernorm(b)
            base = LN_LINKS * NB

            ROUTE_LINKS = 94

            def route(b):
                link = Link(v, dve_link, base + b * ROUTE_LINKS)
                v.wait_ge(sig_ready, b + 1)
                v.wait_ge(y_added, b * (CPB * NE) + 2)
                link(nc.vector.tensor_tensor(sfc[:], score[:], gbias[:].unsqueeze(1).broadcast_to([P, TB, E]),
                                             ALU.add))
                s4 = sfc[:].rearrange("p t (g e) -> p t g e", e=EPG)
                link.put(nc.vector.tensor_tensor(top[:, 0], s4[:, :, :, 0], s4[:, :, :, 1], ALU.max))
                link.put(nc.vector.tensor_tensor(top[:, 1], s4[:, :, :, 0], s4[:, :, :, 1], ALU.min))
                link.put(nc.vector.tensor_tensor(top[:, 2], s4[:, :, :, 2], s4[:, :, :, 3], ALU.max))
                link(nc.vector.tensor_tensor(top[:, 3], s4[:, :, :, 2], s4[:, :, :, 3], ALU.min))
                link.put(nc.vector.tensor_tensor(top[:, 4], top[:, 0], top[:, 2], ALU.max))
                link.put(nc.vector.tensor_tensor(top[:, 5], top[:, 0], top[:, 2], ALU.min))
                link(nc.vector.tensor_tensor(top[:, 6], top[:, 1], top[:, 3], ALU.max))
                link(nc.vector.tensor_tensor(top[:, 5], top[:, 5], top[:, 6], ALU.max))
                link.put(nc.vector.memset(top[:, 1], 0.0))
                link(nc.vector.tensor_tensor(top[:, 0], top[:, 4], top[:, 5], ALU.add))

                def add_ranks(vals, cmp, count, width):
                    for d in range(1, width):
                        n = width - d
                        link(nc.vector.tensor_tensor(cmp[:, :, 0:n], vals[:, :, 0:n], vals[:, :, d:width],
                                                     ALU.is_ge))
                        link.put(nc.vector.tensor_tensor(count[:, :, d:width], count[:, :, d:width],
                                                         cmp[:, :, 0:n], ALU.add))
                        link.wait()
                        link.put(nc.vector.tensor_tensor(count[:, :, 0:n], count[:, :, 0:n], cmp[:, :, 0:n],
                                                         ALU.subtract))
                        link.wait()

                add_ranks(top[:, 0], top[:, 2], top[:, 1], NG)
                for g in range(NG):
                    link.put(nc.vector.tensor_scalar(top[:, 3, :, g:g + 1], top[:, 1, :, g:g + 1],
                                                     float(TG - (NG - 1 - g)), None, ALU.is_lt))
                link.wait()
                link(nc.vector.tensor_scalar(top[:, 4], top[:, 3], -1.0, 3.0e38, ALU.add, ALU.mult))
                b3 = top[:, 3].unsqueeze(3).broadcast_to([P, TB, NG, EPG])
                b4 = top[:, 4].unsqueeze(3).broadcast_to([P, TB, NG, EPG])
                link(nc.vector.tensor_tensor(s4, s4, b3, ALU.mult))
                link.put(nc.vector.memset(rank[:], 0.0))
                link(nc.vector.tensor_tensor(s4, s4, b4, ALU.add))
                add_ranks(sfc[:], beats[:], rank[:], E)
                for e in range(E):
                    link.put(nc.vector.tensor_scalar(beats[:, :, e:e + 1], rank[:, :, e:e + 1],
                                                     float(TOPK - (E - 1 - e)), None, ALU.is_lt))
                link.wait()
                link(nc.vector.tensor_tensor(cw[:], beats[:], score[:], ALU.mult))
                link(nc.vector.tensor_reduce(wsum[:], cw[:], AX.X, ALU.add))
                link(nc.vector.tensor_scalar(wsum[:], wsum[:], 1e-20, None, ALU.add))
                link(nc.vector.reciprocal(wsum[:], wsum[:]))
                link(nc.vector.tensor_scalar(wsum[:], wsum[:], ROUTE_SCALE, None, ALU.mult))
                nc.vector.tensor_tensor(cw[:], cw[:], wsum[:].unsqueeze(2).broadcast_to([P, TB, E]), ALU.mult)\
                    .then_inc(cw_ready, 1)
                assert link.n == ROUTE_LINKS, link.n

            v.wait_ge(w_in, 80)
            with v.Fori(0, NB) as b:
                for half in range(CPB):
                    v.wait_ge(t_done, 2 * b + half + 2)
                    nc.vector.tensor_copy(xT[:, 1, half * CH:(half + 1) * CH], yy[:, 1, :]).then_inc(xT_dve, 1)
                    if half == 0:
                        v.wait_ge(v_stored, 16 * b + 16)
                    for k in range(half * CT, half * CT + CT):
                        v.wait_ge(v_ready, TB * b + k + 1)
                        nc.vector.tensor_tensor(
                            vst[:, :, k, :, 0:HD],
                            yy[:, 2 + k % 2, 0:D].rearrange("p (g j d) -> p g j d", g=GPB, j=HPG),
                            bv[:].rearrange("p (g j d) -> p g j d", g=GPB, j=HPG), ALU.add)
                        nc.vector.tensor_copy(logit[:, k, :], yy[:, 2 + k % 2, D:D + E]).then_inc(v_copied, 1)
                route(b)
                with v.Fori(0, CPB) as c:
                    first = b * (CPB * NE) + c * NE
                    for e in range(NE + 1):
                        n = first + e
                        if e < NE:
                            v.wait_ge(silu_done, n + 1 + 2)
                            v.wait_ge(u_ready, n + 1)
                            v.wait_ge(y_ready, n + 1)
                            nc.vector.tensor_tensor(act[:, e % 2], sg[:, e % 2], gu[:, 2 + e % 2], ALU.mult)\
                                .then_inc(act_done, 1)
                        if e > 0:
                            v.wait_ge(y_ready, n + 2)
                            v.wait_ge(y_added, n - 1 + 2)
                            if e == 1:
                                v.wait_ge(cw_ready, b + 1)
                                v.wait_ge(g_done, b * CPB + c + 1)
                            q = (e - 1) % 2
                            for k in range(CT):
                                yk = yy[:, 2 * q + k // 2, (k % 2) * D:(k % 2 + 1) * D]
                                so_far = yacc[:, k, :]
                                if e == 1:
                                    so_far = xg[:, ds(b * TB + c * CT + k, 1), :].rearrange("p a d -> p (a d)")
                                weight = cw[:, ds(c * CT + k, 1), e - 1] if e <= E else 1.0
                                ins = nc.vector.scalar_tensor_tensor(yacc[:, k, :], yk, weight, so_far,
                                                                     ALU.mult, ALU.add)
                            ins.then_inc(y_added, 1)

        @block.tensor
        def _(pe):
            pe.sem_inc(t_done, 1)
            pe.sem_inc(y_ready, 2)
            pe.wait_ge(ident_ready, 1)
            pe.wait_ge(w_in, 80)
            with pe.Fori(0, NB) as b:
                pe.wait_ge(xnb_ready, b + 1)
                pe.wait_ge(y_added, b * (CPB * NE) + 2)
                for half in range(CPB):
                    for k in range(CT):
                        for c in range(KC):
                            ins = nc.tensor.transpose(yy[:, c, k * P:(k + 1) * P],
                                                      xnb[:, half * CT + k, c * P:(c + 1) * P], ident[:])
                    ins.then_inc(t_done, 1)
                    pe.wait_ge(xT_act, 2 * b + half + 1)
                    pe.wait_ge(xT_dve, 2 * b + half + 1)
                    for k in range(half * CT, half * CT + CT):
                        pe.wait_ge(v_copied, TB * b + k + 1)
                        for c in range(KC):
                            ins = nc.tensor.matmul(yy[:, 2 + k % 2, 0:D + E], xT[:, c, k * P:(k + 1) * P],
                                                   wvg[:, c, :], start=(c == 0), stop=(c == KC - 1))
                        ins.then_inc(v_ready, 1)
                for n in range(2 * 4):
                    half, m = n // 4, n % 4
                    pe.wait_ge(qk_copied, 8 * b + n + 1)
                    for c in range(KC):
                        ins = nc.tensor.matmul(gu[:, n % 4], wqk[:, c, m * P:(m + 1) * P],
                                               xT[:, c, half * CH:(half + 1) * CH],
                                               start=(c == 0), stop=(c == KC - 1))
                    ins.then_inc(qk_ready, 1)
                with pe.Fori(0, CPB) as ch:
                    pe.wait_ge(qk_copied, 8 * b + 8 + 4)
                    pe.wait_ge(v_copied, TB * b + TB + 2)
                    pe.wait_ge(wffn_in, 48)
                    for e in range(NE + 1):
                        n = b * (CPB * NE) + ch * NE + e
                        if e < NE:
                            for w, bank, free, ready in ((wg, 0, silu_done, g_ready), (wu, 2, act_done, u_ready)):
                                pe.wait_ge(free, n + 1)
                                for c in range(KC):
                                    ins = nc.tensor.matmul(gu[:, bank + e % 2], w[:, c, e * I:(e + 1) * I],
                                                           xT[:, c, ds(ch * CH, CH)],
                                                           start=(c == 0), stop=(c == KC - 1))
                                ins.then_inc(ready, 1)
                        if e > 0:
                            pe.wait_ge(act_done, n + 2)
                            pe.wait_ge(y_added, n)
                            q = (e - 1) % 2
                            for k in range(CT):
                                ins = nc.tensor.matmul(yy[:, 2 * q + k // 2, (k % 2) * D:(k % 2 + 1) * D],
                                                       act[:, q, k * P:(k + 1) * P], wd[:, e - 1, :],
                                                       start=True, stop=True)
                            ins.then_inc(y_ready, 1)


def attention(nc, t, scr, o_all, xin, ident, x_in):
    with ExitStack() as ctx:
        sb = lambda name, shape, dt=F32: ctx.enter_context(nc.sbuf_tensor(name, shape, dt))
        sem = lambda name: ctx.enter_context(nc.semaphore(name))
        ident16 = sb("ident16", [P, P], BF16)
        qs = sb("qs", [P, 3, HPG, T], BF16)
        ks = sb("ks", [P, 3, HPG, T], BF16)
        vg = sb("vg", [P, 3, KT, HPG, VW])
        NP = 8
        prob = sb("prob", [P, NP, CH])
        mx = sb("mx", [P, 2, TB])
        zero = sb("zero", [P, TB])
        mrest = sb("mrest", [P, 2, TB])
        mparts = sb("mparts", [P, 2, PARTS, TB], BF16)
        mrows = sb("mrows", [PARTS * TB, 2, P], BF16)
        oT = sb("oT", [P, 2, CH])
        rden = sb("rden", [P, CT, HPG])
        sp_ = ctx.enter_context(nc.psum_tensor("s_rows", [P, 2, T], F32))
        xp = ctx.enter_context(nc.psum_tensor("s_cols", [P, 2, CH], F32))
        pv = ctx.enter_context(nc.psum_tensor("pv", [P, CH], F32))
        mp = ctx.enter_context(nc.psum_tensor("turned", [P, CH], F32))

        ident16_ready = sem("ident16_ready")
        const_ready = sem("const_ready")
        stack_in = [sem(f"stack_in{u}") for u in range(3)]
        v_in = [sem(f"v_in{u}") for u in range(3)]
        s_ready, row_max = sem("s_ready"), sem("row_max")
        mx_split = sem("mx_split")
        pool_link = sem("pool_link")
        turned, turned_read = sem("turned_ready"), sem("turned_read")
        rows_in = sem("rows_in")
        x_ready, exp_done = sem("x_ready"), sem("exp_done")
        pv_done = sem("pv_done")
        pv_copied = sem("pv_copied")
        dve_link = sem("dve_link2")
        block = ctx.enter_context(nc.Block())

        STEPS = 2 * KT
        UNITS = HPG * TB
        SHARE = [3, 2, 3, 2, 3, 2, 3, 2, 3, 2, 3, 2, 2, 0, 0, 0]
        TURN_AT = {4: 0, 8: 1, 11: 2, 14: 3}
        OUT_AT = 9
        TURNS = HPG + 2
        PROLOGUE_TURNS = HPG

        def turn_of_rows(hd):
            return [0, 1, 3, 4][hd]

        def turn_of_out(qh):
            return [2, 5][qh]

        LOOPS = (GROUPS - 1) // 3
        assert LOOPS * 3 == GROUPS - 1

        @block.sync
        def _(sp):
            def load(G, u):
                for i, (qp, kp) in enumerate(PRODUCTS):
                    for side, dst, part in ((0, qs, qp), (1, ks, kp)):
                        sp.dma_start(
                            dst[i * HD:(i + 1) * HD, u],
                            scr["qk"][ds(G, 1), side, part].rearrange("a (j d) t -> d (a j) t", j=HPG),
                        ).then_inc(stack_in[u], 16)
                sp.dma_start(vg[:, u].rearrange("p k j w -> p (k j w)"),
                             scr["v"][ds(G, 1)].rearrange("a p n -> p (a n)")).then_inc(v_in[u], 16)

            for u in range(3):
                load(u, u)
            sp.dma_start(xin[:], t["x"].rearrange("(t p) d -> p t d", p=P)).then_inc(x_in, 16)
            with sp.Fori(0, LOOPS - 1) as it:
                for u in range(3):
                    sp.wait_ge(pv_done, STEPS * (3 * it + u + 1) + 2)
                    load(3 * it + u + 3, u)
            sp.wait_ge(pv_done, STEPS * (GROUPS - 3) + 2)
            load(GROUPS - 1, 0)
            sp.wait_ge(x_in, 16)

        @block.gpsimd
        def _(pool):
            nc.gpsimd.memset(ks[STACK:ROWS].rearrange("r u j t -> r (u j t)"), -1.0).then_inc(const_ready, 1)
            pool.wait_ge(const_ready, 3)
            pool.sem_inc(mx_split, 2)

            def split(G, hd):
                i, head = hd % 2, G * HPG + hd
                pool.wait_ge(row_max, G * UNITS + (hd + 1) * TB + 2)
                if isinstance(G, int) and G == 0:
                    if hd >= 2:
                        pool.wait_ge(turned, hd - 1)
                elif hd >= 2:
                    pool.wait_ge(turned, PROLOGUE_TURNS + TURNS * (G - 1) + turn_of_rows(hd - 2) + 1)
                else:
                    pool.wait_ge(turned, PROLOGUE_TURNS + TURNS * (G - 1))
                link = Link(pool, pool_link, head * 3)
                link(nc.gpsimd.tensor_tensor(mparts[:, i, 0], mx[:, i], zero[:], ALU.add))
                link(nc.gpsimd.tensor_tensor(mrest[:, i], mx[:, i], mparts[:, i, 0], ALU.subtract))
                link(nc.gpsimd.tensor_tensor(mparts[:, i, 1], mrest[:, i], zero[:], ALU.add))
                nc.gpsimd.tensor_tensor(mparts[:, i, 2], mrest[:, i], mparts[:, i, 1], ALU.subtract)\
                    .then_inc(mx_split, 1)

            for hd in range(HPG):
                split(0, hd)
            with pool.Fori(1, GROUPS) as G:
                for hd in range(HPG):
                    split(G, hd)

        @block.scalar
        def _(a):
            a.sem_inc(exp_done, 2)
            a.sem_inc(pv_copied, 1)

            def rows(G, u, hd, use):
                a.wait_ge(turned, use + 1)
                if not (isinstance(G, int) and G == 0 and hd == 0):
                    a.wait_ge(rows_in, 16 * (G * HPG + hd))
                nc.scalar.copy(mrows[:, hd % 2], mp[0:PARTS * TB, 0:P // 2].bitcast(BF16))\
                    .then_inc(turned_read, 1)
                a.wait_ge(turned_read, use + 2)
                a.dma_start(qs[STACK:ROWS, u, hd, :].rearrange("r (k q) -> r k q", q=P),
                            mrows[:, hd % 2]).then_inc(rows_in, 16)

            def copy_pv(G, qh):
                r = 2 * G + qh
                a.wait_ge(pv_done, (r + 1) * KT + 2)
                nc.scalar.copy(oT[:, qh], pv[:]).then_inc(pv_copied, 1)

            def group(G, u, ahead):
                use = PROLOGUE_TURNS + TURNS * G
                for s in range(STEPS):
                    for j in range(HPG):
                        n = G * (STEPS * HPG) + s * HPG + j
                        a.wait_ge(x_ready, n + 1)
                        a.wait_ge(pv_done, G * STEPS + s + 1)
                        nc.scalar.activation(prob[:, (s % 2) * HPG + j], xp[:, j % 2], ACT.Exp,
                                             scale=1.0 / HD ** 0.5).then_inc(exp_done, 1)
                        if s == KT and j == 1:
                            copy_pv(G, 0)
                    if ahead and s in TURN_AT:
                        hd = TURN_AT[s]
                        rows(G + 1, (u + 1) % 3, hd, use + turn_of_rows(hd))
                copy_pv(G, 1)

            for hd in range(HPG):
                rows(0, 0, hd, hd)
            with a.Fori(0, LOOPS) as it:
                for u in range(3):
                    group(3 * it + u, u, True)
            group(GROUPS - 1, 0, False)

        @block.vector
        def _(v):
            nc.vector.memset(pv[:], 0.0).then_inc(const_ready, 1)
            nc.vector.memset(zero[:], 0.0).then_inc(const_ready, 1)
            nc.vector.tensor_copy(ident16[:], ident[:]).then_inc(ident16_ready, 1)
            v.sem_inc(row_max, 2)
            v.sem_inc(turned_read, 1)

            def unit(G, n):
                hd, k = n // TB, n % TB
                if k == 0:
                    v.wait_ge(mx_split, G * HPG + hd + 1)
                v.wait_ge(s_ready, G * UNITS + n + 1)
                nc.vector.tensor_reduce(mx[:, hd % 2, k:k + 1], sp_[:, n % 2, :], AX.X, ALU.max)\
                    .then_inc(row_max, 1)

            def out(G, qh, use):
                link = Link(v, dve_link, 2 * G + qh)
                v.wait_ge(turned, use + 1)
                cols = mp[:].rearrange("p (k j c) -> p k j c", k=CT, j=HPG)
                link(nc.vector.reciprocal(rden[:], cols[:, :, :, HD]))
                nc.vector.tensor_tensor(
                    o_all[:, ds(G, 1), qh * CT:(qh + 1) * CT, :].rearrange("p a k (j d) -> p (a k) j d", j=HPG),
                    cols[:, :, :, 0:HD], rden[:].unsqueeze(3).broadcast_to([P, CT, HPG, HD]), ALU.mult)\
                    .then_inc(turned_read, 1)

            def group(G, ahead):
                use = PROLOGUE_TURNS + TURNS * G
                n = 0
                for s in range(STEPS):
                    if ahead:
                        for _ in range(SHARE[s]):
                            unit(G + 1, n)
                            n += 1
                    if s == OUT_AT:
                        out(G, 0, use + (turn_of_out(0) if ahead else 0))
                out(G, 1, use + (turn_of_out(1) if ahead else 1))

            for n in range(UNITS):
                unit(0, n)
            with v.Fori(0, GROUPS - 1) as G:
                group(G, True)
            group(GROUPS - 1, False)

        @block.tensor
        def _(pe):
            pe.sem_inc(pv_done, 2)
            pe.wait_ge(const_ready, 3)
            pe.wait_ge(ident16_ready, 1)

            def unit(G, u, n):
                hd, k = n // TB, n % TB
                pe.wait_ge(row_max, G * UNITS + n + 1)
                for kh in range(T // CH):
                    ins = nc.tensor.matmul(sp_[:, n % 2, kh * CH:(kh + 1) * CH],
                                           qs[0:STACK, u, hd, k * P:(k + 1) * P],
                                           ks[0:STACK, u, hd, kh * CH:(kh + 1) * CH], start=True, stop=True)
                ins.then_inc(s_ready, 1)

            def turn_rows(G, hd, use):
                pe.wait_ge(mx_split, G * HPG + hd + 1 + 2)
                pe.wait_ge(turned_read, use + 1)
                nc.tensor.transpose(mp[0:PARTS * TB, 0:P // 2].bitcast(BF16),
                                    mparts[:, hd % 2].rearrange("p s k -> p (s k)"), ident16[:])\
                    .then_inc(turned, 1)

            def turn_out(G, qh, use):
                pe.wait_ge(pv_copied, 2 * G + qh + 2)
                pe.wait_ge(turned_read, use + 1)
                for k in range(CT):
                    ins = nc.tensor.transpose(mp[:, k * P:(k + 1) * P], oT[:, qh, k * P:(k + 1) * P], ident[:])
                ins.then_inc(turned, 1)

            def scores(G, u, s, j):
                qh, k = s // KT, s % KT
                pe.wait_ge(exp_done, G * (STEPS * HPG) + s * HPG + j + 1)
                ins = nc.tensor.matmul(xp[:, j % 2], ks[0:ROWS, u, j, k * P:(k + 1) * P],
                                       qs[0:ROWS, u, j, qh * CH:(qh + 1) * CH], start=True, stop=True)
                ins.then_inc(x_ready, 1)
                return ins

            def values(G, u, s):
                qh, k = s // KT, s % KT
                pe.wait_ge(exp_done, G * (STEPS * HPG) + s * HPG + HPG + 2)
                if k == 0:
                    pe.wait_ge(pv_copied, 2 * G + qh + 1)
                for j in range(HPG):
                    ins = nc.tensor.matmul(pv[32 * j:32 * j + VW, :], vg[:, u, k, j, :],
                                           prob[:, (s % 2) * HPG + j], start=(k == 0), stop=(k == KT - 1))
                ins.then_inc(pv_done, 1)

            def group(G, u, it, ahead):
                use = PROLOGUE_TURNS + TURNS * G
                pe.wait_ge(rows_in, 16 * HPG * (G + 1))
                pe.wait_ge(v_in[u], 16 * (it + 1))
                un = (u + 1) % 3
                if ahead:
                    pe.wait_ge(stack_in[un], 16 * 12 * (it + (2 if un == 0 else 1)))
                n = 0
                for s in range(STEPS):
                    scores(G, u, s, 0)
                    scores(G, u, s, 1)
                    if s % KT:
                        values(G, u, s - 1)
                    scores(G, u, s, 2)
                    ins = scores(G, u, s, 3)
                    if ahead:
                        for _ in range(SHARE[s]):
                            unit(G + 1, un, n)
                            n += 1
                    if s % KT == KT - 1:
                        values(G, u, s)
                    if s == OUT_AT:
                        turn_out(G, 0, use + (turn_of_out(0) if ahead else 0))
                    if ahead and s in TURN_AT:
                        turn_rows(G + 1, TURN_AT[s], use + turn_of_rows(TURN_AT[s]))
                turn_out(G, 1, use + (turn_of_out(1) if ahead else 1))

            pe.wait_ge(stack_in[0], 16 * 12)
            for hd in range(HPG):
                for k in range(TB):
                    unit(0, 0, hd * TB + k)
                if hd:
                    turn_rows(0, hd - 1, hd - 1)
            turn_rows(0, HPG - 1, HPG - 1)
            with pe.Fori(0, LOOPS) as it:
                for u in range(3):
                    group(3 * it + u, u, it, True)
            group(GROUPS - 1, 0, LOOPS, False)


def project_out(nc, t, xg, o_all, xin, ident):
    with ExitStack() as ctx:
        sb = lambda name, shape, dt=F32: ctx.enter_context(nc.sbuf_tensor(name, shape, dt))
        sem = lambda name: ctx.enter_context(nc.semaphore(name))
        wo = sb("wo_sb", [P, KC, D])
        bo = sb("bo_sb", [P, D])
        ost = sb("ost", [P, 2, CT, D])
        oT = sb("oT3", [P, 2, KC, CH])
        res = sb("res", [P, 2, CT, D])
        tp = ctx.enter_context(nc.psum_tensor("tp", [P, 2, KC, CH], F32))
        spj = ctx.enter_context(nc.psum_tensor("spj", [P, 2, CT, D], F32))
        w_in = sem("wo_in")
        ost_ready = sem("ost_ready")
        t_done, oT_act, oT_dve = sem("t_done3"), sem("oT_act"), sem("oT_dve")
        s_ready, s_biased, gated = sem("s_ready3"), sem("s_biased"), sem("gated")
        res_ready = sem("res_ready")
        stored = [sem(f"stored{i}") for i in range(2)]
        block = ctx.enter_context(nc.Block())
        ov = t["out"].rearrange("(c k p) d -> c p k d", p=P, k=CT)

        @block.sync
        def _(sp):
            sp.dma_start(wo[:], t["wo"]).then_inc(w_in, 16)
            sp.dma_start(bo[:], t["bo"].to_broadcast([P, D])).then_inc(w_in, 16)
            for s in stored:
                sp.sem_inc(s, 16)
            with sp.Fori(0, NB) as it:
                for i in range(2):
                    c = 2 * it + i
                    sp.wait_ge(res_ready, c + 1)
                    sp.dma_start(ov[ds(c, 1)].rearrange("a p k d -> p (a k) d"), res[:, i]).then_inc(stored[i], 16)
            for i in range(2):
                sp.wait_ge(stored[i], 16 + 16 * NB)

        @block.gpsimd
        def _(pool):
            with pool.Fori(0, NB) as it:
                for i in range(2):
                    c = 2 * it + i
                    pool.wait_ge(s_biased, c + 1 + 2)
                    nc.gpsimd.tensor_tensor(res[:, i], res[:, i], xg[:, ds(c * CT, CT), :], ALU.mult)\
                        .then_inc(gated, 1)

        @block.scalar
        def _(a):
            with a.Fori(0, NB) as it:
                for i in range(2):
                    c = 2 * it + i
                    a.wait_ge(t_done, c + 1)
                    nc.scalar.copy(ost[:, i].rearrange("p k (g w) -> p k g w", g=GPB),
                                   o_all[:, ds(it * GPB, GPB), i * CT:(i + 1) * CT, :].rearrange(
                                       "p g k w -> p k g w")).then_inc(ost_ready, 1)
                    a.wait_ge(t_done, c + 1 + 2)
                    nc.scalar.copy(oT[:, i, 0], tp[:, i, 0]).then_inc(oT_act, 1)

        @block.vector
        def _(v):
            v.sem_inc(s_biased, 2)
            v.wait_ge(w_in, 32)
            with v.Fori(0, NB) as it:
                for i in range(2):
                    c = 2 * it + i
                    v.wait_ge(t_done, c + 1 + 2)
                    nc.vector.tensor_copy(oT[:, i, 1], tp[:, i, 1]).then_inc(oT_dve, 1)
                    v.wait_ge(s_ready, c + 1)
                    v.wait_ge(stored[i], 16 * (it + 1))
                    nc.vector.tensor_tensor(res[:, i], spj[:, i],
                                            bo[:].unsqueeze(1).broadcast_to([P, CT, D]), ALU.add)\
                        .then_inc(s_biased, 1)
                    v.wait_ge(gated, c + 1)
                    nc.vector.tensor_tensor(res[:, i], res[:, i], xin[:, ds(c * CT, CT), :], ALU.add).then_inc(res_ready, 1)

        @block.tensor
        def _(pe):
            pe.sem_inc(t_done, 2)
            pe.wait_ge(w_in, 32)
            with pe.Fori(0, NB) as it:
                for i in range(2):
                    c = 2 * it + i
                    pe.wait_ge(ost_ready, c + 1)
                    for k in range(CT):
                        for h in range(KC):
                            ins = nc.tensor.transpose(tp[:, i, h, k * P:(k + 1) * P],
                                                      ost[:, i, k, h * P:(h + 1) * P], ident[:])
                    ins.then_inc(t_done, 1)
                    pe.wait_ge(oT_act, c + 1)
                    pe.wait_ge(oT_dve, c + 1)
                    pe.wait_ge(s_biased, c + 1)
                    for k in range(CT):
                        for h in range(KC):
                            ins = nc.tensor.matmul(spj[:, i, k], oT[:, i, h, k * P:(k + 1) * P], wo[:, h, :],
                                                   start=(h == 0), stop=(h == KC - 1))
                    ins.then_inc(s_ready, 1)


def build(nc, t):
    with ExitStack() as ctx:
        xg = ctx.enter_context(nc.sbuf_tensor("xg", [P, TILES, D], F32))
        ident = ctx.enter_context(nc.sbuf_tensor("ident", [P, P], F32))
        o_all = ctx.enter_context(nc.sbuf_tensor("o_all", [P, GROUPS, TB, HPG * HD], F32))
        scr = {
            "qk": nc.dram_tensor("qk_parts", [GROUPS, 2, PARTS, HPG * HD, T], BF16).ap(),
            "v": nc.dram_tensor("v_ones", [GROUPS, P, KT * HPG * VW], F32).ap(),
        }
        project_and_ffn(nc, t, scr, xg, ident)
        xin = ctx.enter_context(nc.sbuf_tensor("xin", [P, TILES, D], F32))
        x_in = ctx.enter_context(nc.semaphore("x_in"))
        attention(nc, t, scr, o_all, xin, ident, x_in)
        project_out(nc, t, xg, o_all, xin, ident)


def kernel(**inputs):
    import numpy as np
    import concourse.bacc as bacc
    from concourse.bass_utils import run_bass_kernel_spmd

    a = {k[3:]: np.asarray(v) for k, v in inputs.items()}

    def by_contraction(w):
        return np.ascontiguousarray(w.T.reshape(KC, P, -1).transpose(1, 0, 2))

    def experts(w, shared):
        return by_contraction(np.concatenate([w.reshape(E * I, D), shared]))

    wd = np.concatenate([a["ffn_Wd"].transpose(2, 0, 1), a["ffn_Ws_d"].T.reshape(2, I, D).transpose(1, 0, 2)], 1)
    arrays = {
        "x": a["attn_x"].reshape(N, D),
        "wqk": by_contraction(a["attn_W_qkv"][0:2 * D]),
        "wvg": by_contraction(np.concatenate([a["attn_W_qkv"][2 * D:], a["ffn_gate_w"]])),
        "bqk": np.ascontiguousarray(a["attn_b_qkv"][0:2 * D].reshape(4, P).T),
        "bv": a["attn_b_qkv"][2 * D:].reshape(1, D),
        "gbias": a["ffn_gate_bias"].reshape(1, E),
        "wg": experts(a["ffn_Wg"], a["ffn_Ws_g"]),
        "wu": experts(a["ffn_Wu"], a["ffn_Ws_u"]),
        "wd": np.ascontiguousarray(wd),
        "wo": by_contraction(a["attn_W_o"]),
        "bo": a["attn_b_o"].reshape(1, D),
    }
    nc = bacc.Bacc("TRN2", target_bir_lowering=False, num_devices=1)
    t = {k: nc.dram_tensor(f"{k}_dram", v.shape, F32, kind="ExternalInput").ap() for k, v in arrays.items()}
    t["out"] = nc.dram_tensor("out_dram", (N, D), F32, kind="ExternalOutput").ap()
    build(nc, t)
    r = run_bass_kernel_spmd(nc, [{f"{k}_dram": v for k, v in arrays.items()}], core_ids=[0])
    return r.results[0]["out_dram"].reshape(NB, T, D)
```

```python
from contextlib import ExitStack

import concourse.bass as bass
from concourse import mybir

F32 = mybir.dt.float32
F32R = mybir.dt.float32r
BF16 = mybir.dt.bfloat16
ALU = mybir.AluOpType
ACT = mybir.ActivationFunctionType
AX = mybir.AxisListType

P = 128
NB, T, D = 4, 1024, 256
HEADS, HD = 16, 16
N = NB * T
TILES = N // P
TB = T // P
KC = D // P
E, TOPK, NG, TG = 16, 4, 4, 2
EPG = E // NG
I = 128
NE = E + 2
CH = 512
CT = CH // P
CPB = T // CH
HPG = 4
GROUPS = NB * HEADS // HPG
GPB = HEADS // HPG
VW = HD + 1
KT = T // P
PARTS = 3
STACK = 6 * HD
ROWS = STACK + PARTS
EPS = 1e-5
ROUTE_SCALE = 2.5
PRODUCTS = [(0, 0), (1, 0), (2, 0), (0, 1), (1, 1), (0, 2)]


def ds(start, size):
    return bass.ds(start, size)


class Link:

    def __init__(self, eng, sem, start=0):
        self.eng, self.sem, self.start, self.n = eng, sem, start, 0

    def put(self, ins):
        ins.then_inc(self.sem, 1)
        self.n += 1

    def wait(self):
        self.eng.wait_ge(self.sem, self.start + self.n)

    def __call__(self, ins):
        self.put(ins)
        self.wait()


def project_and_ffn(nc, t, scr, xg, ident):
    with ExitStack() as ctx:
        sb = lambda name, shape, dt=F32: ctx.enter_context(nc.sbuf_tensor(name, shape, dt))
        sem = lambda name: ctx.enter_context(nc.semaphore(name))
        wqk32 = sb("wqk32", [P, KC, 2 * D])
        wqk = [sb(f"wqk{i}", [P, KC, 2 * D], F32R) for i in range(2)]
        wvg = sb("wvg_sb", [P, KC, D + E])
        bqk = sb("bqk_sb", [P, 4])
        bv = sb("bv_sb", [P, D])
        gbias = sb("gbias_sb", [P, E])
        stats = sb("stats", [P, TB, 6])
        ln = sb("ln", [P, 8, TB])
        xnb = sb("xnb", [P, TB, D])
        xTb = sb("xTb", [P, KC, T])
        xT = [sb(f"xT{i}", [P, KC, N], F32R) for i in range(2)]
        qk32 = sb("qk32", [P, 2, CH])
        rest = sb("rest", [P, 2, CH])
        parts = sb("parts", [P, 2, PARTS, CH], BF16)
        vst = sb("vst", [P, GPB, KT, HPG, VW])
        logit = sb("logit", [P, TILES, E])
        score = sb("score", [P, TILES, E])
        sfc = sb("sfc", [P, TILES, E])
        beats = sb("beats", [P, TILES, E])
        rank = sb("rank", [P, TILES, E])
        cw = sb("cw", [P, NE, TILES])
        top = sb("top", [P, 7, TILES, NG])
        wsum = sb("wsum", [P, TILES])
        WG, WU, WD = 0, KC * I, 2 * KC * I
        we32 = sb("we32", [P, 2, 2 * KC * I + D])
        we = [sb(f"we{i}", [P, 2, 2 * KC * I + D], F32R) for i in range(2)]
        sg = sb("sg", [P, 2, CH])
        act32 = sb("act32", [P, 2, CH])
        act = [sb(f"act{i}", [P, 2, CH], F32R) for i in range(2)]
        gu = ctx.enter_context(nc.psum_tensor("gu", [P, 4, 512], F32))
        yy = ctx.enter_context(nc.psum_tensor("yy", [P, 4, 512], F32))
        PASSES = [(0, 0), (1, 0), (0, 1)]

        x_first, x_rest, w_in = sem("x_first"), sem("x_rest"), sem("w_in")
        ident_zero, ident_ready = sem("ident_zero"), sem("ident_ready")
        dve_link = sem("dve_link")
        wqk_high, wqk_ready = sem("wqk_high"), sem("wqk_ready")
        var_ready, std_ready, xn_ready = sem("var_ready"), sem("std_ready"), sem("xn_ready")
        xnb_ready = sem("xnb_ready")
        t_done = sem("t_done")
        xTb_ready = sem("xTb_ready")
        xT_high, xT_ready = sem("xT_high"), sem("xT_ready")
        v_ready, v_copied = sem("v_ready"), sem("v_copied")
        v_stored = sem("v_stored")
        qk_ready, qk_copied = sem("qk_ready"), sem("qk_copied")
        rest_ready, mid_ready, split_done = sem("rest_ready"), sem("mid_ready"), sem("split_done")
        parts_stored = [sem(f"parts_stored{i}") for i in range(2)]
        sig_ready, cw_ready = sem("sig_ready"), sem("cw_ready")
        we_in = [sem(f"we_in{i}") for i in range(2)]
        we_high = sem("we_high")
        we_ready = sem("we_ready")
        g_ready, u_ready = sem("g_ready"), sem("u_ready")
        silu_done, act_done = sem("silu_done"), sem("act_done")
        act_high, act_low = sem("act_high"), sem("act_low")
        y_ready, y_added = sem("y_ready"), sem("y_added")
        block = ctx.enter_context(nc.Block())

        CHUNKS = N // CH
        PAIRS = NE // 2
        PAIR_STEPS = 2 * CHUNKS
        STEPS = PAIRS * PAIR_STEPS
        SPLIT_AT = 2
        QK_AT = {4 * m + 1: m for m in range(4)}

        def v_bank(k):
            return (yy, gu)[k % 4 // 2][:, 2 + k % 2]

        def tile_of(c):
            return (c % NB * CPB + c // NB) * CT

        @block.sync
        def _(sp):
            xv = t["x"].rearrange("(t p) d -> p t d", p=P)
            sp.dma_start(xg[:, 0:TB, :], xv[:, 0:TB, :]).then_inc(x_first, 16)
            sp.dma_start(wvg[:], t["wvg"]).then_inc(w_in, 16)
            sp.dma_start(bqk[:], t["bqk"]).then_inc(w_in, 16)
            sp.dma_start(bv[:], t["bv"].to_broadcast([P, D])).then_inc(w_in, 16)
            sp.dma_start(gbias[:], t["gbias"].to_broadcast([P, E])).then_inc(w_in, 16)
            for b in range(1, NB):
                if b > 1:
                    sp.wait_ge(x_rest, 16 * (b - 1))
                sp.dma_start(xg[:, b * TB:(b + 1) * TB, :], xv[:, b * TB:(b + 1) * TB, :]).then_inc(x_rest, 16)
                if b == 1:
                    sp.dma_start(wqk32[:], t["wqk"]).then_inc(w_in, 16)
                    for i in range(2):
                        sp.dma_start(we32[:, i], t["we"][i]).then_inc(we_in[i], 16)
            sp.sem_inc(v_stored, 16)
            for s in parts_stored:
                sp.sem_inc(s, 32)
            with sp.Fori(0, NB) as b:
                sp.wait_ge(v_copied, TB * b + TB + 4)
                sp.dma_start(scr["v"][ds(b * GPB, GPB)].rearrange("g p n -> p g n"),
                             vst[:].rearrange("p g k j w -> p g (k j w)")).then_inc(v_stored, 16)

            def load_expert(pair, i):
                sp.wait_ge(we_ready, 2 * pair + i + 1)
                sp.dma_start(we32[:, i], t["we"][ds(2 * pair + i, 1)].rearrange("a p n -> p (a n)"))\
                    .then_inc(we_in[i], 16)

            def store_parts(pair, m):
                sp.wait_ge(split_done, 4 * (pair - 1) + m + 1)
                for i in range(2):
                    sp.dma_start(
                        scr["qk"][ds(GPB * (pair - 1) + (m % 2) * 2 + i, 1), m // 2].rearrange(
                            "a s r t -> r (a s) t"),
                        parts[64 * i:64 * i + 64, m % 2],
                    ).then_inc(parts_stored[m % 2], 16)

            load_expert(1, 0)
            load_expert(1, 1)
            with sp.Fori(1, PAIRS - 1) as pair:
                load_expert(pair + 1, 0)
                store_parts(pair, 0)
                load_expert(pair + 1, 1)
                for m in range(1, 4):
                    store_parts(pair, m)
            for m in range(4):
                store_parts(PAIRS - 1, m)
            sp.wait_ge(v_stored, 16 + 16 * NB)
            for s in parts_stored:
                sp.wait_ge(s, 32 + 2 * 32 * CHUNKS)

        @block.gpsimd
        def _(pool):
            nc.gpsimd.memset(ident[:], 0.0).then_inc(ident_zero, 1)
            pool.wait_ge(ident_zero, 1)
            nc.gpsimd.affine_select(out=ident[:], in_=ident[:], compare_op=ALU.not_equal, fill=1.0, base=0,
                                    pattern=[[-1, P]], channel_multiplier=1).then_inc(ident_ready, 1)
            pool.sem_inc(xT_ready, 2)
            with pool.Fori(0, NB) as b:
                for half in range(CPB):
                    pool.wait_ge(xT_high, 2 * b + half + 1)
                    cols = ds((half * NB + b) * CH, CH)
                    nc.gpsimd.tensor_tensor(xT[1][:, :, cols], xTb[:, :, half * CH:(half + 1) * CH],
                                            xT[0][:, :, cols].bitcast(F32), ALU.subtract).then_inc(xT_ready, 1)

            def ffn_pair(pair, first=False):
                for q in range(PAIR_STEPS):
                    n = pair * PAIR_STEPS + q
                    if not (first and q == 0):
                        pool.wait_ge(act_high, n)
                        h = (q - 1) % 2
                        nc.gpsimd.tensor_tensor(act[1][:, h], act32[:, h], act[0][:, h].bitcast(F32),
                                                ALU.subtract).then_inc(act_low, 1)
                    if not first and q - 1 in QK_AT:
                        m = QK_AT[q - 1]
                        pool.wait_ge(qk_copied, 4 * (pair - 1) + m + 1 + 2)
                        nc.gpsimd.tensor_tensor(rest[:, m % 2], qk32[:, m % 2], parts[:, m % 2, 0], ALU.subtract)\
                            .then_inc(rest_ready, 1)
                    if not first and q - 2 in QK_AT:
                        m = QK_AT[q - 2]
                        pool.wait_ge(mid_ready, 4 * (pair - 1) + m + 1)
                        nc.gpsimd.tensor_tensor(parts[:, m % 2, 2], rest[:, m % 2], parts[:, m % 2, 1],
                                                ALU.subtract).then_inc(split_done, 1)

            ffn_pair(0, first=True)
            with pool.Fori(1, PAIRS) as pair:
                ffn_pair(pair)
            pool.wait_ge(act_high, STEPS)
            nc.gpsimd.tensor_tensor(act[1][:, 1], act32[:, 1], act[0][:, 1].bitcast(F32), ALU.subtract)\
                .then_inc(act_low, 1)

        @block.scalar
        def _(a):
            a.sem_inc(qk_copied, 2)
            a.sem_inc(silu_done, 1)

            def std(b):
                a.wait_ge(var_ready, b + 1)
                nc.scalar.activation(ln[:, 3], ln[:, 4], ACT.Sqrt).then_inc(std_ready, 1)

            def turned_x(b, last):
                a.wait_ge(xn_ready, b + 1)
                a.wait_ge(t_done, 2 * b + 1)
                nc.scalar.copy(xnb[:], xg[:, ds(b * TB, TB), :]).then_inc(xnb_ready, 1)
                for half in range(CPB):
                    a.wait_ge(t_done, 2 * b + half + 2)
                    a.wait_ge(xT_ready, 2 * b + half + 1)
                    turned = yy[:, 0:KC, :] if half == 0 else gu[:, 0:KC, :]
                    nc.scalar.copy(xTb[:, :, half * CH:(half + 1) * CH], turned).then_inc(xTb_ready, 1)
                    nc.scalar.copy(xT[0][:, :, ds((half * NB + b) * CH, CH)], turned).then_inc(xT_high, 1)
                    if half == 0 and not last:
                        std(b + 1)

            std(0)
            with a.Fori(0, NB - 1) as b:
                turned_x(b, False)
            turned_x(NB - 1, True)

            def high_weights(pair, i):
                a.wait_ge(we_in[i], 16 * (pair + 1))
                if not (isinstance(pair, int) and pair == 0 and i == 0):
                    a.wait_ge(y_ready, (2 * pair + i - 1) * CHUNKS + 2)
                nc.scalar.copy(we[0][:, i], we32[:, i]).then_inc(we_high, 1)

            high_weights(0, 0)
            a.wait_ge(w_in, 80)
            nc.scalar.copy(wqk[0][:], wqk32[:]).then_inc(wqk_high, 1)
            a.wait_ge(v_copied, TILES + 4)
            nc.scalar.activation(score[:], logit[:], ACT.Sigmoid).then_inc(sig_ready, 1)

            def ffn_pair(pair, first=False, last=False):
                for q in range(PAIR_STEPS):
                    n = pair * PAIR_STEPS + q
                    if q == SPLIT_AT:
                        high_weights(pair, 1)
                    if q == CHUNKS + SPLIT_AT and not last:
                        high_weights(pair + 1, 0)
                    if not (first and q == 0):
                        a.wait_ge(act_done, n + 2)
                        a.wait_ge(y_ready, n)
                        nc.scalar.copy(act[0][:, (q - 1) % 2], act32[:, (q - 1) % 2]).then_inc(act_high, 1)
                    if not first and q - 1 in QK_AT:
                        m = QK_AT[q - 1]
                        a.wait_ge(qk_ready, 4 * (pair - 1) + m + 1)
                        a.wait_ge(parts_stored[m % 2], 32 * (2 * (pair - 1) + m // 2 + 1))
                        nc.scalar.activation(qk32[:, m % 2], gu[:, 2 + m % 2], ACT.Identity, bias=bqk[:, m:m + 1])
                        nc.scalar.activation(parts[:, m % 2, 0], gu[:, 2 + m % 2], ACT.Identity,
                                             bias=bqk[:, m:m + 1]).then_inc(qk_copied, 1)
                    if not first and q - 2 in QK_AT:
                        m = QK_AT[q - 2]
                        a.wait_ge(rest_ready, 4 * (pair - 1) + m + 1)
                        nc.scalar.copy(parts[:, m % 2, 1], rest[:, m % 2]).then_inc(mid_ready, 1)
                    a.wait_ge(g_ready, n + 1)
                    a.wait_ge(act_done, n + 1)
                    nc.scalar.activation(sg[:, q % 2], gu[:, 0], ACT.Silu).then_inc(silu_done, 1)

            ffn_pair(0, first=True)
            with a.Fori(1, PAIRS - 1) as pair:
                ffn_pair(pair)
            ffn_pair(PAIRS - 1, last=True)
            a.wait_ge(act_done, STEPS + 2)
            a.wait_ge(y_ready, STEPS)
            nc.scalar.copy(act[0][:, 1], act32[:, 1]).then_inc(act_high, 1)

        @block.vector
        def _(v):
            nc.vector.memset(vst[:], 1.0)
            nc.vector.memset(cw[:, 0:2, :], 1.0).then_inc(cw_ready, 1)
            v.sem_inc(v_copied, 4)
            v.sem_inc(act_done, 2)
            v.sem_inc(y_added, 2)
            v.sem_inc(we_ready, 2)

            LN_LINKS = 12

            def layernorm(b):
                link = Link(v, dve_link, b * LN_LINKS)
                for k in range(TB):
                    ins = nc.vector.bn_stats(stats[:, k, :], xg[:, b * TB + k, :])
                link(ins)
                even, odd = stats[:, :, 0:3], stats[:, :, 3:6]
                link.put(nc.vector.tensor_tensor(ln[:, 0], even[:, :, 1], odd[:, :, 1], ALU.add))
                link.put(nc.vector.tensor_tensor(ln[:, 1], even[:, :, 1], odd[:, :, 1], ALU.subtract))
                link(nc.vector.tensor_tensor(ln[:, 2], even[:, :, 2], odd[:, :, 2], ALU.add))
                link.put(nc.vector.scalar_tensor_tensor(ln[:, 5], ln[:, 1], 0.25, ln[:, 1], ALU.mult, ALU.mult))
                link.put(nc.vector.tensor_scalar(ln[:, 6], ln[:, 2], 1.0 / D, EPS, ALU.mult, ALU.add))
                link(nc.vector.tensor_scalar(ln[:, 0], ln[:, 0], 0.5, None, ALU.mult))
                nc.vector.tensor_tensor(ln[:, 4], ln[:, 5], ln[:, 6], ALU.add).then_inc(var_ready, 1)
                v.wait_ge(std_ready, b + 1)
                link(nc.vector.reciprocal(ln[:, 5], ln[:, 3]))
                link(nc.vector.tensor_tensor(ln[:, 6], ln[:, 5], ln[:, 5], ALU.mult))
                link(nc.vector.tensor_tensor(ln[:, 6], ln[:, 6], ln[:, 4], ALU.mult))
                link(nc.vector.tensor_scalar(ln[:, 6], ln[:, 6], -0.5, 1.5, ALU.mult, ALU.add))
                link(nc.vector.tensor_tensor(ln[:, 7], ln[:, 5], ln[:, 6], ALU.mult))
                for k in range(TB):
                    row = xg[:, ds(b * TB + k, 1), :].rearrange("p a d -> p (a d)")
                    ins = nc.vector.tensor_scalar(row, row, ln[:, 0, k:k + 1], ln[:, 7, k:k + 1],
                                                  ALU.subtract, ALU.mult)
                ins.then_inc(xn_ready, 1)
                v.wait_ge(xn_ready, b + 1)
                assert link.n == LN_LINKS, link.n

            def add_rank(link, vals, cmp, count, width, d):
                n = width - d
                link(nc.vector.tensor_tensor(cmp[:, :, 0:n], vals[:, :, 0:n], vals[:, :, d:width], ALU.is_ge))
                link(nc.vector.tensor_tensor(count[:, :, d:width], count[:, :, d:width], cmp[:, :, 0:n], ALU.add))
                link(nc.vector.tensor_tensor(count[:, :, 0:n], count[:, :, 0:n], cmp[:, :, 0:n], ALU.subtract))

            def route_groups(link):
                v.wait_ge(sig_ready, 1)
                link(nc.vector.tensor_tensor(sfc[:], score[:], gbias[:].unsqueeze(1).broadcast_to([P, TILES, E]),
                                             ALU.add))
                s4 = sfc[:].rearrange("p t (g e) -> p t g e", e=EPG)
                link.put(nc.vector.tensor_tensor(top[:, 0], s4[:, :, :, 0], s4[:, :, :, 1], ALU.max))
                link.put(nc.vector.tensor_tensor(top[:, 1], s4[:, :, :, 0], s4[:, :, :, 1], ALU.min))
                link.put(nc.vector.tensor_tensor(top[:, 2], s4[:, :, :, 2], s4[:, :, :, 3], ALU.max))
                link(nc.vector.tensor_tensor(top[:, 3], s4[:, :, :, 2], s4[:, :, :, 3], ALU.min))
                link.put(nc.vector.tensor_tensor(top[:, 4], top[:, 0], top[:, 2], ALU.max))
                link.put(nc.vector.tensor_tensor(top[:, 5], top[:, 0], top[:, 2], ALU.min))
                link(nc.vector.tensor_tensor(top[:, 6], top[:, 1], top[:, 3], ALU.max))
                link(nc.vector.tensor_tensor(top[:, 5], top[:, 5], top[:, 6], ALU.max))
                link.put(nc.vector.memset(top[:, 1], 0.0))
                link(nc.vector.tensor_tensor(top[:, 0], top[:, 4], top[:, 5], ALU.add))
                for d in range(1, NG):
                    add_rank(link, top[:, 0], top[:, 2], top[:, 1], NG, d)
                for g in range(NG):
                    link.put(nc.vector.tensor_scalar(top[:, 3, :, g:g + 1], top[:, 1, :, g:g + 1],
                                                     float(TG - (NG - 1 - g)), None, ALU.is_lt))
                link.wait()
                link(nc.vector.tensor_scalar(top[:, 4], top[:, 3], -1.0, 3.0e38, ALU.add, ALU.mult))
                b3 = top[:, 3].unsqueeze(3).broadcast_to([P, TILES, NG, EPG])
                b4 = top[:, 4].unsqueeze(3).broadcast_to([P, TILES, NG, EPG])
                link(nc.vector.tensor_tensor(s4, s4, b3, ALU.mult))
                link.put(nc.vector.memset(rank[:], 0.0))
                link(nc.vector.tensor_tensor(s4, s4, b4, ALU.add))

            def route_weights(link):
                for e in range(E):
                    link.put(nc.vector.tensor_scalar(beats[:, :, e:e + 1], rank[:, :, e:e + 1],
                                                     float(TOPK - (E - 1 - e)), None, ALU.is_lt))
                link.wait()
                link(nc.vector.tensor_tensor(rank[:], beats[:], score[:], ALU.mult))
                link(nc.vector.tensor_reduce(wsum[:], rank[:], AX.X, ALU.add))
                link(nc.vector.tensor_scalar(wsum[:], wsum[:], 1e-20, None, ALU.add))
                link(nc.vector.reciprocal(wsum[:], wsum[:]))
                link(nc.vector.tensor_scalar(wsum[:], wsum[:], ROUTE_SCALE, None, ALU.mult))
                nc.vector.tensor_tensor(cw[:, 2:NE, :].rearrange("p e t -> p t e"), rank[:],
                                        wsum[:].unsqueeze(2).broadcast_to([P, TILES, E]), ALU.mult)\
                    .then_inc(cw_ready, 1)

            def value(b):
                v.wait_ge(v_stored, 16 * b + 16)
                for k in range(TB):
                    bank = v_bank(k)
                    v.wait_ge(v_ready, TB * b + k + 1)
                    nc.vector.tensor_tensor(
                        vst[:, :, k, :, 0:HD],
                        bank[:, 0:D].rearrange("p (g j d) -> p g j d", g=GPB, j=HPG),
                        bv[:].rearrange("p (g j d) -> p g j d", g=GPB, j=HPG), ALU.add)
                    nc.vector.tensor_copy(logit[:, ds(b * TB + k, 1), :].rearrange("p a e -> p (a e)"),
                                          bank[:, D:D + E]).then_inc(v_copied, 1)

            v.wait_ge(x_first, 16)
            layernorm(0)
            with v.Fori(0, NB - 1) as b:
                v.wait_ge(x_rest, 16 * b + 16)
                layernorm(b + 1)
                v.wait_ge(w_in, 80)
                value(b)
            value(NB - 1)

            def low_weights(pair, i):
                v.wait_ge(we_high, 2 * pair + i + 1)
                nc.vector.tensor_tensor(we[1][:, i], we32[:, i], we[0][:, i].bitcast(F32), ALU.subtract)\
                    .then_inc(we_ready, 1)

            def add_y(pair, q):
                n = pair * PAIR_STEPS + q
                v.wait_ge(y_ready, n + 2)
                v.wait_ge(y_added, n - 1 + 2)
                c, h = (q - 1) % CHUNKS, (q - 1) % 2
                for k in range(CT):
                    tile = tile_of(c) + k
                    ins = nc.vector.scalar_tensor_tensor(
                        xg[:, tile, :], yy[:, 2 * h + k // 2, (k % 2) * D:(k % 2 + 1) * D],
                        cw[:, ds(2 * pair + (q - 1) // CHUNKS, 1), tile], xg[:, tile, :], ALU.mult, ALU.add)
                ins.then_inc(y_added, 1)

            def ffn_pair(pair, link=None, last=False):
                for q in range(PAIR_STEPS):
                    n = pair * PAIR_STEPS + q
                    if q == SPLIT_AT:
                        low_weights(pair, 1)
                    if q == CHUNKS + SPLIT_AT and not last:
                        low_weights(pair + 1, 0)
                    v.wait_ge(silu_done, n + 1 + 1)
                    v.wait_ge(u_ready, n + 1)
                    v.wait_ge(y_ready, n + 1)
                    nc.vector.tensor_tensor(act32[:, q % 2], sg[:, q % 2], gu[:, 1], ALU.mult)\
                        .then_inc(act_done, 1)
                    if not (link and q == 0):
                        add_y(pair, q)
                    if link and q > 0:
                        add_rank(link, sfc[:], beats[:], rank[:], E, q)

            low_weights(0, 0)
            v.wait_ge(wqk_high, 1)
            nc.vector.tensor_tensor(wqk[1][:], wqk32[:], wqk[0][:].bitcast(F32), ALU.subtract)\
                .then_inc(wqk_ready, 1)
            link = Link(v, dve_link, LN_LINKS * NB)
            route_groups(link)
            v.wait_ge(cw_ready, 1)
            ffn_pair(0, link)
            route_weights(link)
            v.wait_ge(cw_ready, 2)
            with v.Fori(1, PAIRS - 1) as pair:
                ffn_pair(pair)
            ffn_pair(PAIRS - 1, last=True)
            add_y(PAIRS, 0)

        @block.tensor
        def _(pe):
            pe.sem_inc(t_done, 1)
            pe.sem_inc(y_ready, 2)
            pe.wait_ge(ident_ready, 1)
            with pe.Fori(0, NB) as b:
                pe.wait_ge(xnb_ready, b + 1)
                for half in range(CPB):
                    turned = yy if half == 0 else gu
                    for k in range(CT):
                        for c in range(KC):
                            ins = nc.tensor.transpose(turned[:, c, k * P:(k + 1) * P],
                                                      xnb[:, half * CT + k, c * P:(c + 1) * P], ident[:])
                    ins.then_inc(t_done, 1)
                pe.wait_ge(w_in, 80)
                for k in range(TB):
                    if k % CT == 0:
                        pe.wait_ge(xTb_ready, 2 * b + k // CT + 1)
                    pe.wait_ge(v_copied, TB * b + k + 1)
                    for c in range(KC):
                        ins = nc.tensor.matmul(v_bank(k)[:, 0:D + E], xTb[:, c, k * P:(k + 1) * P],
                                               wvg[:, c, :], start=(c == 0), stop=(c == KC - 1))
                    ins.then_inc(v_ready, 1)
                pe.wait_ge(xT_high, 2 * b + 2)
            pe.wait_ge(v_copied, TILES + 4)
            pe.wait_ge(xT_ready, 2 * NB + 2)

            def three_pass(out, weights, rhs):
                n = 0
                for c in range(KC):
                    for wp, xp in PASSES:
                        ins = nc.tensor.matmul(out, weights(wp, c), rhs(xp, c), start=(n == 0),
                                               stop=(n == KC * len(PASSES) - 1))
                        n += 1
                return ins

            def ffn_pair(pair, first=False):
                for q in range(PAIR_STEPS):
                    n = pair * PAIR_STEPS + q
                    if q % CHUNKS == 0:
                        pe.wait_ge(we_ready, 2 * pair + q // CHUNKS + 1 + 2)
                    c0, i = q % CHUNKS * CH, q // CHUNKS
                    for at, bank, free, count, ready in ((WG, 0, silu_done, n + 1, g_ready),
                                                         (WU, 1, act_done, n + 2, u_ready)):
                        pe.wait_ge(free, count)
                        three_pass(gu[:, bank], lambda wp, c: we[wp][:, i, at + c * I:at + (c + 1) * I],
                                   lambda xp, c: xT[xp][:, c, c0:c0 + CH]).then_inc(ready, 1)
                    if not first and q in QK_AT:
                        m = QK_AT[q]
                        pe.wait_ge(qk_copied, 4 * (pair - 1) + m + 1)
                        three_pass(gu[:, 2 + m % 2], lambda wp, c: wqk[wp][:, c, m * P:(m + 1) * P],
                                   lambda xp, c: xT[xp][:, c, ds((pair - 1) * CH, CH)]).then_inc(qk_ready, 1)
                    if not (first and q == 0):
                        down(n, q)

            def down(n, q):
                pe.wait_ge(act_low, n)
                pe.wait_ge(y_added, n)
                h, i = (q - 1) % 2, (q - 1) // CHUNKS % 2
                for k in range(CT):
                    for m, (wp, ap) in enumerate(PASSES):
                        ins = nc.tensor.matmul(yy[:, 2 * h + k // 2, (k % 2) * D:(k % 2 + 1) * D],
                                               act[ap][:, h, k * P:(k + 1) * P], we[wp][:, i, WD:WD + D],
                                               start=(m == 0), stop=(m == len(PASSES) - 1))
                ins.then_inc(y_ready, 1)

            ffn_pair(0, first=True)
            pe.wait_ge(wqk_ready, 1)
            with pe.Fori(1, PAIRS) as pair:
                ffn_pair(pair)
            down(STEPS, 0)


def attention(nc, t, scr, o_all, xin, ident, x_in):
    with ExitStack() as ctx:
        sb = lambda name, shape, dt=F32: ctx.enter_context(nc.sbuf_tensor(name, shape, dt))
        sem = lambda name: ctx.enter_context(nc.semaphore(name))
        ident16 = sb("ident16", [P, P], BF16)
        qs = sb("qs", [P, 3, HPG, T], BF16)
        ks = sb("ks", [P, 3, HPG, T], BF16)
        vg = sb("vg", [P, 3, KT, HPG, VW])
        NP = 8
        prob = sb("prob", [P, NP, CH])
        mx = sb("mx", [P, 2, TB])
        zero = sb("zero", [P, TB])
        mrest = sb("mrest", [P, 2, TB])
        mparts = sb("mparts", [P, 2, PARTS, TB], BF16)
        mrows = sb("mrows", [PARTS * TB, 2, P], BF16)
        oT = sb("oT", [P, 2, CH])
        rden = sb("rden", [P, CT, HPG])
        sp_ = ctx.enter_context(nc.psum_tensor("s_rows", [P, 2, T], F32))
        xp = ctx.enter_context(nc.psum_tensor("s_cols", [P, 2, CH], F32))
        pv = ctx.enter_context(nc.psum_tensor("pv", [P, CH], F32))
        mp = ctx.enter_context(nc.psum_tensor("turned", [P, CH], F32))

        ident16_ready = sem("ident16_ready")
        const_ready = sem("const_ready")
        stack_in = [sem(f"stack_in{u}") for u in range(3)]
        v_in = [sem(f"v_in{u}") for u in range(3)]
        s_ready, row_max = sem("s_ready"), sem("row_max")
        mx_split = sem("mx_split")
        pool_link = sem("pool_link")
        turned, turned_read = sem("turned_ready"), sem("turned_read")
        rows_in = sem("rows_in")
        x_ready, exp_done = sem("x_ready"), sem("exp_done")
        pv_done = sem("pv_done")
        pv_copied = sem("pv_copied")
        dve_link = sem("dve_link2")
        block = ctx.enter_context(nc.Block())

        STEPS = 2 * KT
        UNITS = HPG * TB
        SHARE = [3, 2, 3, 2, 3, 2, 3, 2, 3, 2, 3, 2, 2, 0, 0, 0]
        UNIT_AT = {0: (0, 0, 0), 2: (1, 0, 1), 3: (1, 1, 1)}
        TURN_AT = {4: 0, 8: 1, 11: 2, 14: 3}
        OUT_AT = 9
        STACK_DMAS = 2 * len(PRODUCTS) * CPB
        TURNS = HPG + 2
        PROLOGUE_TURNS = HPG

        def turn_of_rows(hd):
            return [0, 1, 3, 4][hd]

        def turn_of_out(qh):
            return [2, 5][qh]

        LOOPS = (GROUPS - 1) // 3
        assert LOOPS * 3 == GROUPS - 1

        @block.sync
        def _(sp):
            def load(G, u):
                for i, (qp, kp) in enumerate(PRODUCTS):
                    for side, dst, part in ((0, qs, qp), (1, ks, kp)):
                        for half in range(CPB):
                            sp.dma_start(
                                dst[i * HD:(i + 1) * HD, u, :, half * CH:(half + 1) * CH],
                                scr["qk"][ds(half * GROUPS + G, 1), side, part].rearrange(
                                    "a (j d) t -> d (a j) t", j=HPG),
                            ).then_inc(stack_in[u], 16)
                sp.dma_start(vg[:, u].rearrange("p k j w -> p (k j w)"),
                             scr["v"][ds(G, 1)].rearrange("a p n -> p (a n)")).then_inc(v_in[u], 16)

            for u in range(3):
                load(u, u)
            sp.dma_start(xin[:], t["x"].rearrange("(t p) d -> p t d", p=P)).then_inc(x_in, 16)
            with sp.Fori(0, LOOPS - 1) as it:
                for u in range(3):
                    sp.wait_ge(pv_done, STEPS * (3 * it + u + 1) + 2)
                    load(3 * it + u + 3, u)
            sp.wait_ge(pv_done, STEPS * (GROUPS - 3) + 2)
            load(GROUPS - 1, 0)
            sp.wait_ge(x_in, 16)

        @block.gpsimd
        def _(pool):
            nc.gpsimd.memset(ks[STACK:ROWS].rearrange("r u j t -> r (u j t)"), -1.0).then_inc(const_ready, 1)
            pool.wait_ge(const_ready, 3)
            pool.sem_inc(mx_split, 2)

            def split(G, hd):
                i, head = hd % 2, G * HPG + hd
                pool.wait_ge(row_max, G * UNITS + (hd + 1) * TB + 2)
                if isinstance(G, int) and G == 0:
                    if hd >= 2:
                        pool.wait_ge(turned, hd - 1)
                elif hd >= 2:
                    pool.wait_ge(turned, PROLOGUE_TURNS + TURNS * (G - 1) + turn_of_rows(hd - 2) + 1)
                else:
                    pool.wait_ge(turned, PROLOGUE_TURNS + TURNS * (G - 1))
                link = Link(pool, pool_link, head * 3)
                link(nc.gpsimd.tensor_tensor(mparts[:, i, 0], mx[:, i], zero[:], ALU.add))
                link(nc.gpsimd.tensor_tensor(mrest[:, i], mx[:, i], mparts[:, i, 0], ALU.subtract))
                link(nc.gpsimd.tensor_tensor(mparts[:, i, 1], mrest[:, i], zero[:], ALU.add))
                nc.gpsimd.tensor_tensor(mparts[:, i, 2], mrest[:, i], mparts[:, i, 1], ALU.subtract)\
                    .then_inc(mx_split, 1)

            for hd in range(HPG):
                split(0, hd)
            with pool.Fori(1, GROUPS) as G:
                for hd in range(HPG):
                    split(G, hd)

        @block.scalar
        def _(a):
            a.sem_inc(exp_done, 2)
            a.sem_inc(pv_copied, 1)

            def rows(G, u, hd, use):
                a.wait_ge(turned, use + 1)
                if not (isinstance(G, int) and G == 0 and hd == 0):
                    a.wait_ge(rows_in, 16 * (G * HPG + hd))
                nc.scalar.copy(mrows[:, hd % 2], mp[0:PARTS * TB, 0:P // 2].bitcast(BF16))\
                    .then_inc(turned_read, 1)
                a.wait_ge(turned_read, use + 2)
                a.dma_start(qs[STACK:ROWS, u, hd, :].rearrange("r (k q) -> r k q", q=P),
                            mrows[:, hd % 2]).then_inc(rows_in, 16)

            def copy_pv(G, qh):
                r = 2 * G + qh
                a.wait_ge(pv_done, (r + 1) * KT + 2)
                nc.scalar.copy(oT[:, qh], pv[:]).then_inc(pv_copied, 1)

            def group(G, u, ahead):
                use = PROLOGUE_TURNS + TURNS * G
                for s in range(STEPS):
                    for j in range(HPG):
                        n = G * (STEPS * HPG) + s * HPG + j
                        a.wait_ge(x_ready, n + 1)
                        a.wait_ge(pv_done, G * STEPS + s + 1)
                        nc.scalar.activation(prob[:, (s % 2) * HPG + j], xp[:, j % 2], ACT.Exp,
                                             scale=1.0 / HD ** 0.5).then_inc(exp_done, 1)
                        if s == KT and j == 1:
                            copy_pv(G, 0)
                    if ahead and s in TURN_AT:
                        hd = TURN_AT[s]
                        rows(G + 1, (u + 1) % 3, hd, use + turn_of_rows(hd))
                copy_pv(G, 1)

            for hd in range(HPG):
                rows(0, 0, hd, hd)
            with a.Fori(0, LOOPS) as it:
                for u in range(3):
                    group(3 * it + u, u, True)
            group(GROUPS - 1, 0, False)

        @block.vector
        def _(v):
            nc.vector.memset(pv[:], 0.0).then_inc(const_ready, 1)
            nc.vector.memset(zero[:], 0.0).then_inc(const_ready, 1)
            nc.vector.tensor_copy(ident16[:], ident[:]).then_inc(ident16_ready, 1)
            v.sem_inc(row_max, 2)
            v.sem_inc(turned_read, 1)

            def unit(G, n):
                hd, k = n // TB, n % TB
                if k == 0:
                    v.wait_ge(mx_split, G * HPG + hd + 1)
                v.wait_ge(s_ready, G * UNITS + n + 1)
                nc.vector.tensor_reduce(mx[:, hd % 2, k:k + 1], sp_[:, n % 2, :], AX.X, ALU.max)\
                    .then_inc(row_max, 1)

            def out(G, qh, use):
                link = Link(v, dve_link, 2 * G + qh)
                v.wait_ge(turned, use + 1)
                cols = mp[:].rearrange("p (k j c) -> p k j c", k=CT, j=HPG)
                link(nc.vector.reciprocal(rden[:], cols[:, :, :, HD]))
                nc.vector.tensor_tensor(
                    o_all[:, ds(G, 1), qh * CT:(qh + 1) * CT, :].rearrange("p a k (j d) -> p (a k) j d", j=HPG),
                    cols[:, :, :, 0:HD], rden[:].unsqueeze(3).broadcast_to([P, CT, HPG, HD]), ALU.mult)\
                    .then_inc(turned_read, 1)

            def group(G, ahead):
                use = PROLOGUE_TURNS + TURNS * G
                n = 0
                for s in range(STEPS):
                    if ahead:
                        for _ in range(SHARE[s]):
                            unit(G + 1, n)
                            n += 1
                    if s == OUT_AT:
                        out(G, 0, use + (turn_of_out(0) if ahead else 0))
                out(G, 1, use + (turn_of_out(1) if ahead else 1))

            for n in range(UNITS):
                unit(0, n)
            with v.Fori(0, GROUPS - 1) as G:
                group(G, True)
            group(GROUPS - 1, False)

        @block.tensor
        def _(pe):
            pe.sem_inc(pv_done, 2)
            pe.wait_ge(const_ready, 3)
            pe.wait_ge(ident16_ready, 1)

            def unit(G, u, n):
                hd, k = n // TB, n % TB
                pe.wait_ge(row_max, G * UNITS + n + 1)
                for kh in range(T // CH):
                    ins = nc.tensor.matmul(sp_[:, n % 2, kh * CH:(kh + 1) * CH],
                                           qs[0:STACK, u, hd, k * P:(k + 1) * P],
                                           ks[0:STACK, u, hd, kh * CH:(kh + 1) * CH], start=True, stop=True)
                ins.then_inc(s_ready, 1)

            def turn_rows(G, hd, use):
                pe.wait_ge(mx_split, G * HPG + hd + 1 + 2)
                pe.wait_ge(turned_read, use + 1)
                nc.tensor.transpose(mp[0:PARTS * TB, 0:P // 2].bitcast(BF16),
                                    mparts[:, hd % 2].rearrange("p s k -> p (s k)"), ident16[:])\
                    .then_inc(turned, 1)

            def turn_out(G, qh, use):
                pe.wait_ge(pv_copied, 2 * G + qh + 2)
                pe.wait_ge(turned_read, use + 1)
                for k in range(CT):
                    ins = nc.tensor.transpose(mp[:, k * P:(k + 1) * P], oT[:, qh, k * P:(k + 1) * P], ident[:])
                ins.then_inc(turned, 1)

            def scores(G, u, s, j):
                qh, k = s // KT, s % KT
                pe.wait_ge(exp_done, G * (STEPS * HPG) + s * HPG + j + 1)
                ins = nc.tensor.matmul(xp[:, j % 2], ks[0:ROWS, u, j, k * P:(k + 1) * P],
                                       qs[0:ROWS, u, j, qh * CH:(qh + 1) * CH], start=True, stop=True)
                ins.then_inc(x_ready, 1)
                return ins

            def values(G, u, s):
                qh, k = s // KT, s % KT
                pe.wait_ge(exp_done, G * (STEPS * HPG) + s * HPG + HPG + 2)
                if k == 0:
                    pe.wait_ge(pv_copied, 2 * G + qh + 1)
                for j in range(HPG):
                    ins = nc.tensor.matmul(pv[32 * j:32 * j + VW, :], vg[:, u, k, j, :],
                                           prob[:, (s % 2) * HPG + j], start=(k == 0), stop=(k == KT - 1))
                ins.then_inc(pv_done, 1)

            def group(G, u, it, ahead):
                use = PROLOGUE_TURNS + TURNS * G
                pe.wait_ge(rows_in, 16 * HPG * (G + 1))
                pe.wait_ge(v_in[u], 16 * (it + 1))
                un = (u + 1) % 3
                if ahead:
                    pe.wait_ge(stack_in[un], STACK_DMAS * 16 * (it + (2 if un == 0 else 1)))
                n = 0
                for s in range(STEPS):
                    scores(G, u, s, 0)
                    scores(G, u, s, 1)
                    for k in range(3):
                        if k == 1:
                            if s % KT:
                                values(G, u, s - 1)
                        if k == 2:
                            scores(G, u, s, 2)
                            scores(G, u, s, 3)
                        if ahead and UNIT_AT[SHARE[s]][k]:
                            unit(G + 1, un, n)
                            n += 1
                    if s % KT == KT - 1:
                        values(G, u, s)
                    if s == OUT_AT:
                        turn_out(G, 0, use + (turn_of_out(0) if ahead else 0))
                    if ahead and s in TURN_AT:
                        turn_rows(G + 1, TURN_AT[s], use + turn_of_rows(TURN_AT[s]))
                turn_out(G, 1, use + (turn_of_out(1) if ahead else 1))

            pe.wait_ge(stack_in[0], STACK_DMAS * 16)
            for hd in range(HPG):
                for k in range(TB):
                    unit(0, 0, hd * TB + k)
                if hd:
                    turn_rows(0, hd - 1, hd - 1)
            turn_rows(0, HPG - 1, HPG - 1)
            with pe.Fori(0, LOOPS) as it:
                for u in range(3):
                    group(3 * it + u, u, it, True)
            group(GROUPS - 1, 0, LOOPS, False)


def project_out(nc, t, xg, o_all, xin, ident):
    with ExitStack() as ctx:
        sb = lambda name, shape, dt=F32: ctx.enter_context(nc.sbuf_tensor(name, shape, dt))
        sem = lambda name: ctx.enter_context(nc.semaphore(name))
        wo = sb("wo_sb", [P, KC, D])
        bo = sb("bo_sb", [P, D])
        heads = sb("heads", [P, 2, CT, D])
        oT = sb("oT3", [P, 2, KC, CH])
        gate = sb("gate", [P, 2, CT, D])
        res = sb("res", [P, 2, CT, D])
        tp = ctx.enter_context(nc.psum_tensor("tp", [P, 2, KC, CH], F32))
        spj = ctx.enter_context(nc.psum_tensor("spj", [P, 2, CT, D], F32))
        w_in = sem("wo_in")
        heads_ready = sem("heads_ready")
        t_done, oT_act, oT_dve = sem("t_done3"), sem("oT_act"), sem("oT_dve")
        s_ready, s_biased = sem("s_ready3"), sem("s_biased")
        gate_ready, gated, res_ready = sem("gate_ready"), sem("gated"), sem("res_ready")
        stored = [sem(f"stored{i}") for i in range(2)]
        block = ctx.enter_context(nc.Block())
        ov = t["out"].rearrange("(c k p) d -> c p k d", p=P, k=CT)
        CHUNKS = N // CH

        @block.sync
        def _(sp):
            sp.dma_start(wo[:], t["wo"]).then_inc(w_in, 16)
            sp.dma_start(bo[:], t["bo"].to_broadcast([P, D])).then_inc(w_in, 16)
            for c in range(CHUNKS):
                sp.wait_ge(res_ready, c + 1)
                sp.dma_start(ov[c], res[:, c % 2]).then_inc(stored[c % 2], 16)
            for s in stored:
                sp.wait_ge(s, 16 * CHUNKS // 2)

        @block.gpsimd
        def _(pool):
            for c in range(CHUNKS):
                pool.wait_ge(s_biased, c + 1)
                pool.wait_ge(gate_ready, c + 1)
                nc.gpsimd.tensor_tensor(res[:, c % 2], res[:, c % 2], gate[:, c % 2], ALU.mult).then_inc(gated, 1)

        @block.scalar
        def _(a):
            def gather(c):
                b, first = c // CPB, c % CPB * CT
                if c >= 2:
                    a.wait_ge(t_done, c - 1)
                nc.scalar.copy(heads[:, c % 2].rearrange("p k (g w) -> p k g w", g=GPB),
                               o_all[:, b * GPB:(b + 1) * GPB, first:first + CT, :].rearrange("p g k w -> p k g w"))\
                    .then_inc(heads_ready, 1)

            gather(0)
            gather(1)
            for c in range(CHUNKS):
                if c >= 2:
                    a.wait_ge(gated, c - 1)
                nc.scalar.activation(gate[:, c % 2], xg[:, c * CT:(c + 1) * CT, :], ACT.Silu).then_inc(gate_ready, 1)
                a.wait_ge(t_done, c + 1)
                if c >= 2:
                    a.wait_ge(s_ready, c - 1)
                nc.scalar.copy(oT[:, c % 2, 0], tp[:, c % 2, 0]).then_inc(oT_act, 1)
                if c + 2 < CHUNKS:
                    gather(c + 2)

        @block.vector
        def _(v):
            v.wait_ge(w_in, 32)

            def finish(c):
                v.wait_ge(gated, c + 1)
                nc.vector.tensor_tensor(res[:, c % 2], res[:, c % 2], xin[:, c * CT:(c + 1) * CT, :], ALU.add)\
                    .then_inc(res_ready, 1)

            for c in range(CHUNKS):
                v.wait_ge(t_done, c + 1)
                if c >= 2:
                    v.wait_ge(s_ready, c - 1)
                nc.vector.tensor_copy(oT[:, c % 2, 1], tp[:, c % 2, 1]).then_inc(oT_dve, 1)
                if c >= 1:
                    finish(c - 1)
                v.wait_ge(s_ready, c + 1)
                if c >= 2:
                    v.wait_ge(stored[c % 2], 16 * (c // 2))
                nc.vector.tensor_tensor(res[:, c % 2], spj[:, c % 2],
                                        bo[:].unsqueeze(1).broadcast_to([P, CT, D]), ALU.add)\
                    .then_inc(s_biased, 1)
            finish(CHUNKS - 1)

        @block.tensor
        def _(pe):
            def turn(c):
                if c >= 2:
                    pe.wait_ge(oT_act, c - 1)
                    pe.wait_ge(oT_dve, c - 1)
                pe.wait_ge(heads_ready, c + 1)
                for k in range(CT):
                    for h in range(KC):
                        ins = nc.tensor.transpose(tp[:, c % 2, h, k * P:(k + 1) * P],
                                                  heads[:, c % 2, k, h * P:(h + 1) * P], ident[:])
                ins.then_inc(t_done, 1)

            pe.wait_ge(w_in, 32)
            turn(0)
            for c in range(CHUNKS):
                if c + 1 < CHUNKS:
                    turn(c + 1)
                pe.wait_ge(oT_act, c + 1)
                pe.wait_ge(oT_dve, c + 1)
                if c >= 2:
                    pe.wait_ge(s_biased, c - 1)
                for k in range(CT):
                    for h in range(KC):
                        ins = nc.tensor.matmul(spj[:, c % 2, k], oT[:, c % 2, h, k * P:(k + 1) * P], wo[:, h, :],
                                               start=(h == 0), stop=(h == KC - 1))
                ins.then_inc(s_ready, 1)


def build(nc, t):
    with ExitStack() as ctx:
        xg = ctx.enter_context(nc.sbuf_tensor("xg", [P, TILES, D], F32))
        ident = ctx.enter_context(nc.sbuf_tensor("ident", [P, P], F32))
        scr = {
            "qk": nc.dram_tensor("qk_parts", [CPB * GROUPS, 2, PARTS, HPG * HD, CH], BF16).ap(),
            "v": nc.dram_tensor("v_ones", [GROUPS, P, KT * HPG * VW], F32).ap(),
        }
        project_and_ffn(nc, t, scr, xg, ident)
        o_all = ctx.enter_context(nc.sbuf_tensor("o_all", [P, GROUPS, TB, HPG * HD], F32))
        xin = ctx.enter_context(nc.sbuf_tensor("xin", [P, TILES, D], F32))
        x_in = ctx.enter_context(nc.semaphore("x_in"))
        attention(nc, t, scr, o_all, xin, ident, x_in)
        project_out(nc, t, xg, o_all, xin, ident)


def kernel(**inputs):
    import numpy as np
    import concourse.bacc as bacc
    from concourse.bass_utils import run_bass_kernel_spmd

    a = {k[3:]: np.asarray(v) for k, v in inputs.items()}

    def by_contraction(w):
        return np.ascontiguousarray(w.T.reshape(KC, P, -1).transpose(1, 0, 2))

    def experts(w, shared):
        w = np.concatenate([shared.reshape(-1, I, D), w])
        return w.transpose(0, 2, 1).reshape(-1, KC, P, I).transpose(0, 2, 1, 3).reshape(-1, P, KC * I)

    wd = np.concatenate([a["ffn_Ws_d"].T.reshape(-1, I, D), a["ffn_Wd"].transpose(0, 2, 1)])
    arrays = {
        "x": a["attn_x"].reshape(N, D),
        "wqk": by_contraction(a["attn_W_qkv"][0:2 * D]),
        "wvg": by_contraction(np.concatenate([a["attn_W_qkv"][2 * D:], a["ffn_gate_w"]])),
        "bqk": np.ascontiguousarray(a["attn_b_qkv"][0:2 * D].reshape(4, P).T),
        "bv": a["attn_b_qkv"][2 * D:].reshape(1, D),
        "gbias": a["ffn_gate_bias"].reshape(1, E),
        "we": np.concatenate([experts(a["ffn_Wg"], a["ffn_Ws_g"]), experts(a["ffn_Wu"], a["ffn_Ws_u"]), wd], 2),
        "wo": by_contraction(a["attn_W_o"]),
        "bo": a["attn_b_o"].reshape(1, D),
    }
    nc = bacc.Bacc("TRN2", target_bir_lowering=False, num_devices=1)
    t = {k: nc.dram_tensor(f"{k}_dram", v.shape, F32, kind="ExternalInput").ap() for k, v in arrays.items()}
    t["out"] = nc.dram_tensor("out_dram", (N, D), F32, kind="ExternalOutput").ap()
    build(nc, t)
    r = run_bass_kernel_spmd(nc, [{f"{k}_dram": v for k, v in arrays.items()}], core_ids=[0])
    return r.results[0]["out_dram"].reshape(NB, T, D)
```

```python
import struct
from contextlib import ExitStack

import concourse.bass as bass
from concourse import mybir

F32 = mybir.dt.float32
F32R = mybir.dt.float32r
BF16 = mybir.dt.bfloat16
ALU = mybir.AluOpType
ACT = mybir.ActivationFunctionType
AX = mybir.AxisListType

P = 128
NB, T, D = 4, 1024, 256
HEADS, HD = 16, 16
N = NB * T
TILES = N // P
TB = T // P
KC = D // P
E, TOPK, NG, TG = 16, 4, 4, 2
EPG = E // NG
I = 128
NE = E + 2
CH = 512
CT = CH // P
CPB = T // CH
HPG = 4
GROUPS = NB * HEADS // HPG
GPB = HEADS // HPG
VW = HD + 1
KT = T // P
PARTS = 3
STACK = 6 * HD
ROWS = STACK + PARTS
EPS = 1e-5
ROUTE_SCALE = 2.5
PASSES = [(0, 0), (1, 0), (0, 1)]
RUNS = [(0, 0, 0, 3), (3, 1, 0, 2), (5, 2, 0, 1)]
HEADS_BEFORE = HPG + 1
STACK_DMAS = 2 * len(RUNS) * CPB
VST = GPB * KT * HPG * VW


def ds(start, size):
    return bass.ds(start, size)


class Link:

    def __init__(self, eng, sem, start=0):
        self.eng, self.sem, self.start, self.n = eng, sem, start, 0

    def put(self, ins):
        ins.then_inc(self.sem, 1)
        self.n += 1

    def wait(self):
        self.eng.wait_ge(self.sem, self.start + self.n)

    def __call__(self, ins):
        self.put(ins)
        self.wait()


def load_stacks(sp, scr, G, q_stack, k_stack, done):
    for half in range(CPB):
        for row, qp, kp, n in RUNS:
            for side, dst, part in ((0, q_stack, qp), (1, k_stack, kp)):
                sp.dma_start(
                    dst[row * HD:(row + n) * HD, :, half * CH:(half + 1) * CH],
                    scr["qk"][ds(half * GROUPS + G, 1), side, part:part + n].rearrange(
                        "a s (d j) t -> (a s d) j t", j=HPG),
                ).then_inc(done, 16)


def stack_views(stacks):
    both = stacks[:, 0:HPG * T].bitcast(BF16).rearrange("p (s j t) -> p s j t", s=2, j=HPG)
    return both[:, 0], both[:, 1]


def project_and_ffn(nc, t, scr, xg, stack0, stack1, mx0, ident):
    with ExitStack() as ctx:
        sb = lambda name, shape, dt=F32: ctx.enter_context(nc.sbuf_tensor(name, shape, dt))
        sem = lambda name: ctx.enter_context(nc.semaphore(name))
        wqk32 = sb("wqk32", [P, KC, 2 * D])
        wqk = [sb(f"wqk{i}", [P, KC, 2 * D], F32R) for i in range(2)]
        wvg = sb("wvg_sb", [P, KC, D + E])
        bqk = sb("bqk_sb", [P, 4])
        bv = sb("bv_sb", [P, D])
        gbias = sb("gbias_sb", [P, E])
        stats = sb("stats", [P, TB, 6])
        ln = sb("ln", [P, 8, TB])
        xnb = stack0[:, 0:TB * D].rearrange("p (k d) -> p k d", k=TB)
        xTb = stack0[:, TB * D:2 * TB * D].rearrange("p (c t) -> p c t", c=KC)
        vst = stack1[:, 0:VST].rearrange("p (g k j w) -> p g k j w", g=GPB, k=KT, j=HPG)
        qk32 = stack1[:, VST:VST + 2 * CH].rearrange("p (i n) -> p i n", i=2)
        rest = stack1[:, VST + 2 * CH:VST + 4 * CH].rearrange("p (i n) -> p i n", i=2)
        xT = [sb(f"xT{i}", [P, KC, N], F32R) for i in range(2)]
        parts = sb("parts", [P, 2, PARTS, CH], BF16)
        logit = sb("logit", [P, TILES, E])
        score = sb("score", [P, TILES, E])
        sfc = sb("sfc", [P, TILES, E])
        beats = sb("beats", [P, TILES, E], BF16)
        rank = sb("rank", [P, TILES, E], BF16)
        cw = sb("cw", [P, NE, TILES])
        top = sb("top", [P, 7, TILES, NG])
        wsum = sb("wsum", [P, TILES])
        WG, WU, WD = 0, KC * I, 2 * KC * I
        we32 = sb("we32", [P, 2, 2 * KC * I + D])
        we = [sb(f"we{i}", [P, 2, 2 * KC * I + D], F32R) for i in range(2)]
        sg = sb("sg", [P, 2, CH])
        act32 = sb("act32", [P, 2, CH])
        act = [sb(f"act{i}", [P, 2, CH], F32R) for i in range(2)]
        gu = ctx.enter_context(nc.psum_tensor("gu", [P, 4, 512], F32))
        yy = ctx.enter_context(nc.psum_tensor("yy", [P, 4, 512], F32))

        x_first, x_rest, w_in = sem("x_first"), sem("x_rest"), sem("w_in")
        ident_zero, ident_ready = sem("ident_zero"), sem("ident_ready")
        dve_link = sem("dve_link")
        wqk_high, wqk_ready = sem("wqk_high"), sem("wqk_ready")
        var_ready, std_ready, xn_ready = sem("var_ready"), sem("std_ready"), sem("xn_ready")
        xnb_ready = sem("xnb_ready")
        t_done = sem("t_done")
        xTb_ready = sem("xTb_ready")
        xT_high, xT_ready = sem("xT_high"), sem("xT_ready")
        v_ready, v_copied = sem("v_ready"), sem("v_copied")
        v_stored = sem("v_stored")
        qk_ready, qk_copied = sem("qk_ready"), sem("qk_copied")
        rest_ready, mid_ready, split_done = sem("rest_ready"), sem("mid_ready"), sem("split_done")
        parts_stored = [sem(f"parts_stored{i}") for i in range(2)]
        sig_ready, cw_ready = sem("sig_ready"), sem("cw_ready")
        we_in = [sem(f"we_in{i}") for i in range(2)]
        we_high = sem("we_high")
        we_ready = sem("we_ready")
        g_ready, u_ready = sem("g_ready"), sem("u_ready")
        silu_done, act_done = sem("silu_done"), sem("act_done")
        act_high, act_low = sem("act_high"), sem("act_low")
        y_ready, y_added = sem("y_ready"), sem("y_added")
        stack0_in, stack1_in = sem("stack0_in"), sem("stack1_in")
        s_ready, row_max = sem("s0_ready"), sem("row0_max")
        block = ctx.enter_context(nc.Block())

        CHUNKS = N // CH
        PAIRS = NE // 2
        PAIR_STEPS = 2 * CHUNKS
        STEPS = PAIRS * PAIR_STEPS
        SPLIT_AT = 2
        QK_AT = {min(2 * m, PAIR_STEPS - 3): m for m in range(8)}
        FIRST_UNIT = STEPS - HEADS_BEFORE * TB
        UNITS_FROM = FIRST_UNIT // PAIR_STEPS

        def over_pairs(eng, ffn_pair):
            ffn_pair(0, "routing")
            with eng.Fori(1, NB + 1) as pair:
                ffn_pair(pair, "projections")
            with eng.Fori(NB + 1, UNITS_FROM) as pair:
                ffn_pair(pair, "nothing")
            for pair in range(UNITS_FROM, PAIRS):
                ffn_pair(pair, "maxima")

        def is_last(pair):
            return isinstance(pair, int) and pair == PAIRS - 1

        def v_bank(k):
            return (yy, gu)[k % 4 // 2][:, 2 + k % 2]

        def high(m):
            return PARTS - 1 if m % 4 < 2 else 0

        def tile_of(c):
            return (c % NB * CPB + c // NB) * CT

        @block.sync
        def _(sp):
            xv = t["x"].rearrange("(t p) d -> p t d", p=P)
            sp.dma_start(xg[:, 0:TB, :], xv[:, 0:TB, :]).then_inc(x_first, 16)
            sp.dma_start(wvg[:], t["wvg"]).then_inc(w_in, 16)
            sp.dma_start(bqk[:], t["bqk"]).then_inc(w_in, 16)
            sp.dma_start(bv[:], t["bv"].to_broadcast([P, D])).then_inc(w_in, 16)
            sp.dma_start(gbias[:], t["gbias"].to_broadcast([P, E])).then_inc(w_in, 16)
            for b in range(1, NB):
                if b > 1:
                    sp.wait_ge(x_rest, 16 * (b - 1))
                sp.dma_start(xg[:, b * TB:(b + 1) * TB, :], xv[:, b * TB:(b + 1) * TB, :]).then_inc(x_rest, 16)
                if b == 1:
                    sp.dma_start(wqk32[:], t["wqk"]).then_inc(w_in, 16)
                    for i in range(2):
                        sp.dma_start(we32[:, i], t["we"][i]).then_inc(we_in[i], 16)
            sp.sem_inc(v_stored, 16)
            for s in parts_stored:
                sp.sem_inc(s, 32)
            with sp.Fori(0, NB) as b:
                sp.wait_ge(v_copied, TB * b + TB + 4)
                sp.dma_start(scr["v"][ds(b * GPB, GPB)].rearrange("g p n -> p g n"),
                             vst.rearrange("p g k j w -> p g (k j w)")).then_inc(v_stored, 16)

            def load_expert(pair, i):
                sp.wait_ge(we_ready, 2 * pair + i + 1)
                sp.dma_start(we32[:, i], t["we"][ds(2 * pair + i, 1)].rearrange("a p n -> p (a n)"))\
                    .then_inc(we_in[i], 16)

            def store_parts(pair, m):
                sp.wait_ge(split_done, 8 * (pair - 1) + m + 1)
                for i in range(2):
                    group = m // 4 * GROUPS + GPB * (pair - 1) + m % 2 * 2 + i
                    sp.dma_start(
                        scr["qk"][ds(group, 1), m % 4 // 2].rearrange("a s r t -> r (a s) t"),
                        parts[64 * i:64 * i + 64, m % 2],
                    ).then_inc(parts_stored[m % 2], 16)

            def ffn_pair(pair, beside):
                if isinstance(pair, int) and pair == UNITS_FROM:
                    for s in parts_stored:
                        sp.wait_ge(s, 32 + 32 * 4 * NB)
                    sp.wait_ge(xT_ready, 2 * NB + 2)
                    sp.wait_ge(v_copied, TILES + 4)
                    load_stacks(sp, scr, 0, *stack_views(stack0), stack0_in)
                    sp.wait_ge(v_stored, 16 + 16 * NB)
                    load_stacks(sp, scr, 1, *stack_views(stack1), stack1_in)
                if not is_last(pair):
                    load_expert(pair + 1, 0)
                if beside == "projections":
                    store_parts(pair, 0)
                if not is_last(pair):
                    load_expert(pair + 1, 1)
                if beside == "projections":
                    for m in range(1, 8):
                        store_parts(pair, m)

            over_pairs(sp, ffn_pair)
            sp.wait_ge(stack1_in, 16 * STACK_DMAS)

        @block.gpsimd
        def _(pool):
            nc.gpsimd.memset(ident[:], 0.0).then_inc(ident_zero, 1)
            pool.wait_ge(ident_zero, 1)
            nc.gpsimd.affine_select(out=ident[:], in_=ident[:], compare_op=ALU.not_equal, fill=1.0, base=0,
                                    pattern=[[-1, P]], channel_multiplier=1).then_inc(ident_ready, 1)
            pool.sem_inc(xT_ready, 2)
            with pool.Fori(0, NB) as b:
                for half in range(CPB):
                    pool.wait_ge(xT_high, 2 * b + half + 1)
                    cols = ds((half * NB + b) * CH, CH)
                    nc.gpsimd.tensor_tensor(xT[1][:, :, cols], xTb[:, :, half * CH:(half + 1) * CH],
                                            xT[0][:, :, cols].bitcast(F32), ALU.subtract).then_inc(xT_ready, 1)
            pool.wait_ge(wqk_high, 1)
            nc.gpsimd.tensor_tensor(wqk[1][:], wqk32[:], wqk[0][:].bitcast(F32), ALU.subtract)\
                .then_inc(wqk_ready, 1)

            def ffn_pair(pair, beside):
                for q in range(PAIR_STEPS):
                    n = pair * PAIR_STEPS + q
                    if not (beside == "routing" and q == 0):
                        pool.wait_ge(act_high, n)
                        h = (q - 1) % 2
                        nc.gpsimd.tensor_tensor(act[1][:, h], act32[:, h], act[0][:, h].bitcast(F32),
                                                ALU.subtract).then_inc(act_low, 1)
                    if beside == "projections" and q - 1 in QK_AT:
                        m = QK_AT[q - 1]
                        pool.wait_ge(qk_copied, 8 * (pair - 1) + m + 1 + 2)
                        nc.gpsimd.tensor_tensor(rest[:, m % 2], qk32[:, m % 2], parts[:, m % 2, high(m)], ALU.subtract)\
                            .then_inc(rest_ready, 1)
                    if beside == "projections" and q - 2 in QK_AT:
                        m = QK_AT[q - 2]
                        pool.wait_ge(mid_ready, 8 * (pair - 1) + m + 1)
                        nc.gpsimd.tensor_tensor(parts[:, m % 2, PARTS - 1 - high(m)], rest[:, m % 2], parts[:, m % 2, 1],
                                                ALU.subtract).then_inc(split_done, 1)

            over_pairs(pool, ffn_pair)
            pool.wait_ge(act_high, STEPS)
            nc.gpsimd.tensor_tensor(act[1][:, 1], act32[:, 1], act[0][:, 1].bitcast(F32), ALU.subtract)\
                .then_inc(act_low, 1)

        @block.scalar
        def _(a):
            a.sem_inc(qk_copied, 2)
            a.sem_inc(silu_done, 1)

            def std(b):
                a.wait_ge(var_ready, b + 1)
                nc.scalar.activation(ln[:, 3], ln[:, 4], ACT.Sqrt).then_inc(std_ready, 1)

            def turned_x(b, last):
                a.wait_ge(xn_ready, b + 1)
                a.wait_ge(t_done, 2 * b + 1)
                nc.scalar.copy(xnb, xg[:, ds(b * TB, TB), :]).then_inc(xnb_ready, 1)
                if not last:
                    std(b + 1)
                for half in range(CPB):
                    a.wait_ge(t_done, 2 * b + half + 2)
                    a.wait_ge(xT_ready, 2 * b + half + 1)
                    turned = yy[:, 0:KC, :] if half == 0 else gu[:, 0:KC, :]
                    nc.scalar.copy(xTb[:, :, half * CH:(half + 1) * CH], turned).then_inc(xTb_ready, 1)
                    nc.scalar.copy(xT[0][:, :, ds((half * NB + b) * CH, CH)], turned).then_inc(xT_high, 1)

            std(0)
            with a.Fori(0, NB - 1) as b:
                turned_x(b, False)
            turned_x(NB - 1, True)

            def high_weights(pair, i):
                a.wait_ge(we_in[i], 16 * (pair + 1))
                if not (isinstance(pair, int) and pair == 0 and i == 0):
                    a.wait_ge(y_ready, (2 * pair + i - 1) * CHUNKS + 2)
                nc.scalar.copy(we[0][:, i], we32[:, i]).then_inc(we_high, 1)

            high_weights(0, 0)
            a.wait_ge(w_in, 80)
            nc.scalar.copy(wqk[0][:], wqk32[:]).then_inc(wqk_high, 1)
            a.wait_ge(v_copied, TILES + 4)
            nc.scalar.activation(score[:], logit[:], ACT.Sigmoid).then_inc(sig_ready, 1)

            def ffn_pair(pair, beside):
                for q in range(PAIR_STEPS):
                    n = pair * PAIR_STEPS + q
                    if q == SPLIT_AT:
                        high_weights(pair, 1)
                    if q == CHUNKS + SPLIT_AT and not is_last(pair):
                        high_weights(pair + 1, 0)
                    if not (beside == "routing" and q == 0):
                        a.wait_ge(act_done, n + 2)
                        a.wait_ge(y_ready, n)
                        nc.scalar.copy(act[0][:, (q - 1) % 2], act32[:, (q - 1) % 2]).then_inc(act_high, 1)
                    if beside == "projections" and q - 1 in QK_AT:
                        m = QK_AT[q - 1]
                        bias = bqk[:, m % 4:m % 4 + 1]
                        a.wait_ge(qk_ready, 8 * (pair - 1) + m + 1)
                        a.wait_ge(parts_stored[m % 2], 32 * (4 * (pair - 1) + m // 2 + 1))
                        nc.scalar.activation(qk32[:, m % 2], gu[:, 2 + m % 2], ACT.Identity, bias=bias)
                        nc.scalar.activation(parts[:, m % 2, high(m)], gu[:, 2 + m % 2], ACT.Identity, bias=bias)\
                            .then_inc(qk_copied, 1)
                    if beside == "projections" and q - 2 in QK_AT:
                        m = QK_AT[q - 2]
                        a.wait_ge(rest_ready, 8 * (pair - 1) + m + 1)
                        nc.scalar.copy(parts[:, m % 2, 1], rest[:, m % 2]).then_inc(mid_ready, 1)
                    a.wait_ge(g_ready, n + 1)
                    a.wait_ge(act_done, n + 1)
                    nc.scalar.activation(sg[:, q % 2], gu[:, 0], ACT.Silu).then_inc(silu_done, 1)

            over_pairs(a, ffn_pair)
            a.wait_ge(act_done, STEPS + 2)
            a.wait_ge(y_ready, STEPS)
            nc.scalar.copy(act[0][:, 1], act32[:, 1]).then_inc(act_high, 1)

        @block.vector
        def _(v):
            nc.vector.memset(vst, 1.0)
            nc.vector.memset(cw[:, 0:2, :], 1.0).then_inc(cw_ready, 1)
            v.sem_inc(v_copied, 4)
            v.sem_inc(row_max, 1)
            v.sem_inc(act_done, 2)
            v.sem_inc(y_added, 2)
            v.sem_inc(we_ready, 2)

            LN_LINKS = 12

            def route(link, q):
                experts_from = NG + 1
                if q == 0:
                    group_scores(link)
                elif q < NG:
                    add_rank(link, top[:, 0], top[:, 2], top[:, 1], NG, q)
                elif q == NG:
                    mask_groups(link)
                else:
                    steps = PAIR_STEPS - experts_from
                    for d in range(1, E):
                        if (d - 1) * steps // (E - 1) == q - experts_from:
                            add_rank(link, sfc[:], beats[:], rank[:], E, d)
                if q == PAIR_STEPS - 1:
                    route_weights(link)
                    v.wait_ge(cw_ready, 2)

            def statistics(b, k):
                row = xg[:, ds(b * TB + k, 1), :].rearrange("p a d -> p (a d)")
                return nc.vector.bn_stats(stats[:, k, :], row)

            def normalise(b, last_statistics):
                link = Link(v, dve_link, b * LN_LINKS)
                link(last_statistics)
                even, odd = stats[:, :, 0:3], stats[:, :, 3:6]
                link.put(nc.vector.tensor_tensor(ln[:, 0], even[:, :, 1], odd[:, :, 1], ALU.add))
                link.put(nc.vector.tensor_tensor(ln[:, 1], even[:, :, 1], odd[:, :, 1], ALU.subtract))
                link(nc.vector.tensor_tensor(ln[:, 2], even[:, :, 2], odd[:, :, 2], ALU.add))
                link.put(nc.vector.scalar_tensor_tensor(ln[:, 5], ln[:, 1], 0.25, ln[:, 1], ALU.mult, ALU.mult))
                link.put(nc.vector.tensor_scalar(ln[:, 6], ln[:, 2], 1.0 / D, EPS, ALU.mult, ALU.add))
                link(nc.vector.tensor_scalar(ln[:, 0], ln[:, 0], 0.5, None, ALU.mult))
                nc.vector.tensor_tensor(ln[:, 4], ln[:, 5], ln[:, 6], ALU.add).then_inc(var_ready, 1)
                v.wait_ge(std_ready, b + 1)
                link(nc.vector.reciprocal(ln[:, 5], ln[:, 3]))
                link(nc.vector.tensor_tensor(ln[:, 6], ln[:, 5], ln[:, 5], ALU.mult))
                link(nc.vector.tensor_tensor(ln[:, 6], ln[:, 6], ln[:, 4], ALU.mult))
                link(nc.vector.tensor_scalar(ln[:, 6], ln[:, 6], -0.5, 1.5, ALU.mult, ALU.add))
                link(nc.vector.tensor_tensor(ln[:, 7], ln[:, 5], ln[:, 6], ALU.mult))
                for k in range(TB):
                    row = xg[:, ds(b * TB + k, 1), :].rearrange("p a d -> p (a d)")
                    ins = nc.vector.tensor_scalar(row, row, ln[:, 0, k:k + 1], ln[:, 7, k:k + 1],
                                                  ALU.subtract, ALU.mult)
                ins.then_inc(xn_ready, 1)
                v.wait_ge(xn_ready, b + 1)
                assert link.n == LN_LINKS, link.n

            def add_rank(link, vals, cmp, count, width, d):
                n = width - d
                link(nc.vector.tensor_tensor(cmp[:, :, 0:n], vals[:, :, 0:n], vals[:, :, d:width], ALU.is_ge))
                link(nc.vector.tensor_tensor(count[:, :, d:width], count[:, :, d:width], cmp[:, :, 0:n], ALU.add))
                link(nc.vector.tensor_tensor(count[:, :, 0:n], count[:, :, 0:n], cmp[:, :, 0:n], ALU.subtract))

            def group_scores(link):
                v.wait_ge(sig_ready, 1)
                link(nc.vector.tensor_tensor(sfc[:], score[:], gbias[:].unsqueeze(1).broadcast_to([P, TILES, E]),
                                             ALU.add))
                s4 = sfc[:].rearrange("p t (g e) -> p t g e", e=EPG)
                link.put(nc.vector.tensor_tensor(top[:, 0], s4[:, :, :, 0], s4[:, :, :, 1], ALU.max))
                link.put(nc.vector.tensor_tensor(top[:, 1], s4[:, :, :, 0], s4[:, :, :, 1], ALU.min))
                link.put(nc.vector.tensor_tensor(top[:, 2], s4[:, :, :, 2], s4[:, :, :, 3], ALU.max))
                link(nc.vector.tensor_tensor(top[:, 3], s4[:, :, :, 2], s4[:, :, :, 3], ALU.min))
                link.put(nc.vector.tensor_tensor(top[:, 4], top[:, 0], top[:, 2], ALU.max))
                link.put(nc.vector.tensor_tensor(top[:, 5], top[:, 0], top[:, 2], ALU.min))
                link(nc.vector.tensor_tensor(top[:, 6], top[:, 1], top[:, 3], ALU.max))
                link(nc.vector.tensor_tensor(top[:, 5], top[:, 5], top[:, 6], ALU.max))
                link.put(nc.vector.memset(top[:, 1], 0.0))
                link(nc.vector.tensor_tensor(top[:, 0], top[:, 4], top[:, 5], ALU.add))

            def mask_groups(link):
                s4 = sfc[:].rearrange("p t (g e) -> p t g e", e=EPG)
                for g in range(NG):
                    link.put(nc.vector.tensor_scalar(top[:, 3, :, g:g + 1], top[:, 1, :, g:g + 1],
                                                     float(TG - (NG - 1 - g)), None, ALU.is_lt))
                link.wait()
                link(nc.vector.tensor_scalar(top[:, 4], top[:, 3], -1.0, 3.0e38, ALU.add, ALU.mult))
                b3 = top[:, 3].unsqueeze(3).broadcast_to([P, TILES, NG, EPG])
                b4 = top[:, 4].unsqueeze(3).broadcast_to([P, TILES, NG, EPG])
                link(nc.vector.tensor_tensor(s4, s4, b3, ALU.mult))
                link.put(nc.vector.memset(rank[:], 0.0))
                link(nc.vector.tensor_tensor(s4, s4, b4, ALU.add))

            def route_weights(link):
                for e in range(E):
                    link.put(nc.vector.tensor_scalar(beats[:, :, e:e + 1], rank[:, :, e:e + 1],
                                                     float(TOPK - (E - 1 - e)), None, ALU.is_lt))
                link.wait()
                link(nc.vector.tensor_tensor(sfc[:], beats[:], score[:], ALU.mult))
                link(nc.vector.tensor_reduce(wsum[:], sfc[:], AX.X, ALU.add))
                link(nc.vector.tensor_scalar(wsum[:], wsum[:], 1e-20, None, ALU.add))
                link(nc.vector.reciprocal(wsum[:], wsum[:]))
                link(nc.vector.tensor_scalar(wsum[:], wsum[:], ROUTE_SCALE, None, ALU.mult))
                nc.vector.tensor_tensor(cw[:, 2:NE, :].rearrange("p e t -> p t e"), sfc[:],
                                        wsum[:].unsqueeze(2).broadcast_to([P, TILES, E]), ALU.mult)\
                    .then_inc(cw_ready, 1)

            def value(b, k):
                bank = v_bank(k)
                v.wait_ge(v_ready, TB * b + k + 1)
                nc.vector.tensor_tensor(
                    vst[:, :, k, :, 0:HD],
                    bank[:, 0:D].rearrange("p (g j d) -> p g j d", g=GPB, j=HPG),
                    bv[:].rearrange("p (g j d) -> p g j d", g=GPB, j=HPG), ALU.add)
                nc.vector.tensor_copy(logit[:, ds(b * TB + k, 1), :].rearrange("p a e -> p (a e)"),
                                      bank[:, D:D + E]).then_inc(v_copied, 1)

            v.wait_ge(x_first, 16)
            for b in range(2):
                if b:
                    v.wait_ge(x_rest, 16)
                for k in range(TB):
                    ins = statistics(b, k)
                normalise(b, ins)
            v.wait_ge(w_in, 80)
            with v.Fori(0, NB - 2) as b:
                v.wait_ge(v_stored, 16 * b + 16)
                v.wait_ge(x_rest, 16 * b + 32)
                for k in range(TB):
                    value(b, k)
                    ins = statistics(b + 2, k)
                normalise(b + 2, ins)
            with v.Fori(NB - 2, NB) as b:
                v.wait_ge(v_stored, 16 * b + 16)
                for k in range(TB):
                    value(b, k)

            def low_weights(pair, i):
                v.wait_ge(we_high, 2 * pair + i + 1)
                nc.vector.tensor_tensor(we[1][:, i], we32[:, i], we[0][:, i].bitcast(F32), ALU.subtract)\
                    .then_inc(we_ready, 1)

            def add_y(pair, q):
                n = pair * PAIR_STEPS + q
                v.wait_ge(y_ready, n + 2)
                v.wait_ge(y_added, n - 1 + 2)
                c, h = (q - 1) % CHUNKS, (q - 1) % 2
                for k in range(CT):
                    tile = tile_of(c) + k
                    ins = nc.vector.scalar_tensor_tensor(
                        xg[:, tile, :], yy[:, 2 * h + k // 2, (k % 2) * D:(k % 2 + 1) * D],
                        cw[:, ds(2 * pair + (q - 1) // CHUNKS, 1), tile], xg[:, tile, :], ALU.mult, ALU.add)
                ins.then_inc(y_added, 1)

            def take_maximum(n):
                v.wait_ge(s_ready, n + 1)
                nc.vector.tensor_reduce(mx0[:, n // TB, n % TB:n % TB + 1], gu[:, 2:4, :], AX.XY, ALU.max)\
                    .then_inc(row_max, 1)

            def ffn_pair(pair, beside):
                for q in range(PAIR_STEPS):
                    n = pair * PAIR_STEPS + q
                    if q == SPLIT_AT:
                        low_weights(pair, 1)
                    if q == CHUNKS + SPLIT_AT and not is_last(pair):
                        low_weights(pair + 1, 0)
                    v.wait_ge(silu_done, n + 1 + 1)
                    v.wait_ge(u_ready, n + 1)
                    v.wait_ge(y_ready, n + 1)
                    nc.vector.tensor_tensor(act32[:, q % 2], sg[:, q % 2], gu[:, 1], ALU.mult)\
                        .then_inc(act_done, 1)
                    if beside == "maxima" and n >= FIRST_UNIT:
                        take_maximum(n - FIRST_UNIT)
                    if not (beside == "routing" and q == 0):
                        add_y(pair, q)
                    if beside == "routing":
                        route(link, q)

            low_weights(0, 0)
            link = Link(v, dve_link, LN_LINKS * NB)
            v.wait_ge(cw_ready, 1)
            over_pairs(v, ffn_pair)
            add_y(PAIRS, 0)

        @block.tensor
        def _(pe):
            pe.sem_inc(t_done, 1)
            pe.sem_inc(y_ready, 2)
            pe.wait_ge(ident_ready, 1)
            with pe.Fori(0, NB) as b:
                pe.wait_ge(xnb_ready, b + 1)
                for half in range(CPB):
                    turned = yy if half == 0 else gu
                    for k in range(CT):
                        for c in range(KC):
                            ins = nc.tensor.transpose(turned[:, c, k * P:(k + 1) * P],
                                                      xnb[:, half * CT + k, c * P:(c + 1) * P], ident[:])
                    ins.then_inc(t_done, 1)
                pe.wait_ge(w_in, 80)
                for k in range(TB):
                    if k % CT == 0:
                        pe.wait_ge(xTb_ready, 2 * b + k // CT + 1)
                    pe.wait_ge(v_copied, TB * b + k + 1)
                    for c in range(KC):
                        ins = nc.tensor.matmul(v_bank(k)[:, 0:D + E], xTb[:, c, k * P:(k + 1) * P],
                                               wvg[:, c, :], start=(c == 0), stop=(c == KC - 1))
                    ins.then_inc(v_ready, 1)
                pe.wait_ge(xT_high, 2 * b + 2)
            pe.wait_ge(v_copied, TILES + 4)
            pe.wait_ge(xT_ready, 2 * NB + 2)

            def three_pass(out, weights, rhs):
                n = 0
                for c in range(KC):
                    for wp, xp in PASSES:
                        ins = nc.tensor.matmul(out, weights(wp, c), rhs(xp, c), start=(n == 0),
                                               stop=(n == KC * len(PASSES) - 1))
                        n += 1
                return ins

            def unit(n):
                q_stack, k_stack = stack_views((stack0, stack1)[n // (HPG * TB)])
                hd, k = n // TB % HPG, n % TB
                if n % (HPG * TB) == 0:
                    pe.wait_ge((stack0_in, stack1_in)[n // (HPG * TB)], 16 * STACK_DMAS)
                pe.wait_ge(row_max, n + 1)
                for kh in range(T // CH):
                    ins = nc.tensor.matmul(gu[:, 2 + kh], q_stack[0:STACK, hd, k * P:(k + 1) * P],
                                           k_stack[0:STACK, hd, kh * CH:(kh + 1) * CH], start=True, stop=True)
                ins.then_inc(s_ready, 1)

            def ffn_pair(pair, beside):
                if beside == "projections":
                    pe.wait_ge(wqk_ready, 1)
                if beside == "maxima":
                    pe.wait_ge(qk_copied, 8 * NB + 2)
                for q in range(PAIR_STEPS):
                    n = pair * PAIR_STEPS + q
                    if q % CHUNKS == 0:
                        pe.wait_ge(we_ready, 2 * pair + q // CHUNKS + 1 + 2)
                    c0, i = q % CHUNKS * CH, q // CHUNKS
                    for at, bank, free, count, ready in ((WG, 0, silu_done, n + 1, g_ready),
                                                         (WU, 1, act_done, n + 2, u_ready)):
                        pe.wait_ge(free, count)
                        three_pass(gu[:, bank], lambda wp, c: we[wp][:, i, at + c * I:at + (c + 1) * I],
                                   lambda xp, c: xT[xp][:, c, c0:c0 + CH]).then_inc(ready, 1)
                    if beside == "projections" and q in QK_AT:
                        m = QK_AT[q]
                        rows, chunk = m % 4 * P, m // 4 * NB + pair - 1
                        pe.wait_ge(qk_copied, 8 * (pair - 1) + m + 1)
                        three_pass(gu[:, 2 + m % 2], lambda wp, c: wqk[wp][:, c, rows:rows + P],
                                   lambda xp, c: xT[xp][:, c, ds(chunk * CH, CH)]).then_inc(qk_ready, 1)
                    if beside == "maxima" and n >= FIRST_UNIT:
                        unit(n - FIRST_UNIT)
                    if not (beside == "routing" and q == 0):
                        down(n, q)

            def down(n, q):
                pe.wait_ge(act_low, n)
                pe.wait_ge(y_added, n)
                h, i = (q - 1) % 2, (q - 1) // CHUNKS % 2
                for k in range(CT):
                    for m, (wp, ap) in enumerate(PASSES):
                        ins = nc.tensor.matmul(yy[:, 2 * h + k // 2, (k % 2) * D:(k % 2 + 1) * D],
                                               act[ap][:, h, k * P:(k + 1) * P], we[wp][:, i, WD:WD + D],
                                               start=(m == 0), stop=(m == len(PASSES) - 1))
                ins.then_inc(y_ready, 1)

            over_pairs(pe, ffn_pair)
            down(STEPS, 0)


def attention(nc, t, scr, stack0, stack1, mx0, o_all, xin, wo, bo, ident):
    with ExitStack() as ctx:
        sb = lambda name, shape, dt=F32: ctx.enter_context(nc.sbuf_tensor(name, shape, dt))
        sem = lambda name: ctx.enter_context(nc.semaphore(name))
        ident16 = sb("ident16", [P, P], BF16)
        stacks = [stack0, stack1, sb("stack2", [P, HPG * T])]
        qs, ks = zip(*[stack_views(x) for x in stacks])
        vg = sb("vg", [P, 3, KT, HPG, VW])
        prob = sb("prob", [P, 2 * HPG, CH])
        mx_half = sb("mx_half", [P, 2, CPB, TB])
        mx = sb("mx", [P, 2, TB])
        zero = sb("zero", [P, TB])
        mrest = sb("mrest", [P, 2, TB])
        mparts = sb("mparts", [P, 2, PARTS, TB], BF16)
        mrows = sb("mrows", [PARTS * TB, HPG, P], BF16)
        oT = sb("oT", [P, 2, CH])
        rden = sb("rden", [P, CT, HPG])
        srow = ctx.enter_context(nc.psum_tensor("s_rows", [P, 3, CH], F32))
        xp = ctx.enter_context(nc.psum_tensor("s_cols", [P, 3, CH], F32))
        pv = ctx.enter_context(nc.psum_tensor("pv", [P, CH], F32))
        mp = ctx.enter_context(nc.psum_tensor("turned", [P, CH], F32))

        ident16_ready = sem("ident16_ready")
        zero_ready, pv_zero = sem("zero_ready"), sem("pv_zero")
        minus_ready = sem("minus_ready")
        x_in = sem("x_in")
        stack_in = [sem(f"stack_in{u}") for u in range(3)]
        v_in = [sem(f"v_in{u}") for u in range(3)]
        s_ready, half_max = sem("s_ready"), sem("half_max")
        row_max = sem("row_max")
        mx_split = sem("mx_split")
        pool_link = sem("pool_link")
        turned, turned_read = sem("turned_ready"), sem("turned_read")
        rows_in = [sem(f"rows_in{hd}") for hd in range(HPG)]
        x_ready, exp_done = sem("x_ready"), sem("exp_done")
        pv_done = sem("pv_done")
        pv_copied = sem("pv_copied")
        dve_link = sem("dve_link2")
        block = ctx.enter_context(nc.Block())

        STEPS = 2 * KT
        UNITS = HPG * TB
        AHEAD = 2 * STEPS * (HPG - 1) // HPG

        def units_of(G, s):
            units = [(1, n + TB) if n < AHEAD else (2, n - AHEAD) for n in (2 * s, 2 * s + 1)]
            return [(ahead, n) for ahead, n in units if exists(G + ahead)]

        def stack_loads(u, use, ahead):
            return use + (u + ahead) // 3 + (1 if (u + ahead) % 3 == 2 else 0)

        TURN_AT = {1: 0, 5: 1, 9: 2, 13: 3}
        LAST_OUT_AT, OUT_AT = 2, 10
        PROLOGUE_TURNS = HPG
        TURNS = HPG + 2

        def turn_of_rows(G, hd):
            if first(G):
                return PROLOGUE_TURNS + [0, 1, 2, 4][hd]
            return PROLOGUE_TURNS - 1 + TURNS * G + [0, 2, 3, 5][hd]

        def turn_of_out(G, qh):
            if exists(G + 1):
                return PROLOGUE_TURNS - 1 + TURNS * G + (4 if qh == 0 else TURNS + 1 - (not exists(G + 2)))
            return PROLOGUE_TURNS - 1 + TURNS * G + (1 if qh == 0 else 2)

        LOOPS = (GROUPS - 4) // 3
        assert LOOPS * 3 == GROUPS - 4

        def over_groups(eng, group):
            group(0, 0, 0)
            with eng.Fori(0, LOOPS) as it:
                group(3 * it + 1, 1, it)
                group(3 * it + 2, 2, it)
                group(3 * it + 3, 0, it + 1)
            for G in range(GROUPS - 3, GROUPS):
                group(G, G % 3, G // 3)

        def last(G):
            return isinstance(G, int) and G == GROUPS - 1

        def x_bank(G, u, s, j):
            if last(G):
                return xp[:, j] if j < 3 else srow[:, 0]
            return xp[:, (u + s + j) % 3]

        def half_bank(u, n, half):
            return srow[:, (u + 2 + 2 * n + half) % 3]

        def first(G):
            return isinstance(G, int) and G == 0

        def exists(G):
            return not isinstance(G, int) or G < GROUPS

        @block.sync
        def _(sp):
            def load_values(G, u):
                sp.dma_start(vg[:, u].rearrange("p k j w -> p (k j w)"),
                             scr["v"][ds(G, 1)].rearrange("a p n -> p (a n)")).then_inc(v_in[u], 16)

            def load(G, u):
                load_stacks(sp, scr, G, qs[u], ks[u], stack_in[u])
                load_values(G, u)

            load_values(0, 0)
            load_values(1, 1)

            def store_rows(G, u, hd, use):
                sp.wait_ge(turned_read, use + 2)
                sp.dma_start(qs[u][STACK:ROWS, hd, :].rearrange("r (k q) -> r k q", q=P),
                             mrows[:, hd]).then_inc(rows_in[hd], 16)

            def group(G, u, use):
                if not first(G) and exists(G + 2):
                    sp.wait_ge(pv_done, STEPS * G + 2)
                    load(G + 2, (u + 2) % 3)
                if exists(G + 1):
                    for hd in range(HPG):
                        store_rows(G + 1, (u + 1) % 3, hd, turn_of_rows(G, hd))

            for hd in range(HPG):
                store_rows(0, 0, hd, hd)
            load(2, 2)
            sp.dma_start(xin[:], t["x"].rearrange("(t p) d -> p t d", p=P)).then_inc(x_in, 16)
            sp.dma_start(wo[:], t["wo"]).then_inc(x_in, 16)
            sp.dma_start(bo[:], t["bo"].to_broadcast([P, D])).then_inc(x_in, 16)
            over_groups(sp, group)
            sp.wait_ge(x_in, 48)

        @block.gpsimd
        def _(pool):
            pool.sem_inc(mx_split, 2)
            pool.wait_ge(zero_ready, 1)

            def split(G, hd):
                i, head = hd % 2, G * HPG + hd
                before = isinstance(G, int) and G * HPG + hd < HEADS_BEFORE
                maxima = mx0[:, G * HPG + hd] if before else mx[:, i]
                if not before:
                    pool.wait_ge(row_max, G * HPG + hd + 1 - HEADS_BEFORE)
                if isinstance(G, int) and G == 0:
                    if hd >= 2:
                        pool.wait_ge(turned, hd - 1)
                elif isinstance(G, int) and G == 1 and hd < 2:
                    pool.wait_ge(turned, hd + 3)
                elif hd >= 2:
                    pool.wait_ge(turned, turn_of_rows(G - 1, hd - 2) + 1)
                else:
                    pool.wait_ge(turned, turn_of_rows(G - 2, hd + 2) + 1)
                link = Link(pool, pool_link, head * 3)
                link(nc.gpsimd.tensor_tensor(mparts[:, i, 0], maxima, zero[:], ALU.add))
                link(nc.gpsimd.tensor_tensor(mrest[:, i], maxima, mparts[:, i, 0], ALU.subtract))
                link(nc.gpsimd.tensor_tensor(mparts[:, i, 1], mrest[:, i], zero[:], ALU.add))
                nc.gpsimd.tensor_tensor(mparts[:, i, 2], mrest[:, i], mparts[:, i, 1], ALU.subtract)\
                    .then_inc(mx_split, 1)

            for hd in range(HPG):
                split(0, hd)
            pool.wait_ge(mx_split, HPG + 2)
            minus_pair = struct.unpack("f", struct.pack("I", 0xBF80BF80))[0]
            for u in range(3):
                nc.gpsimd.memset(ks[u][STACK:ROWS].rearrange("r j t -> r (j t)").bitcast(F32), minus_pair)\
                    .then_inc(minus_ready, 1)
                pool.wait_ge(minus_ready, u + 1)
            for G in range(1, 3):
                for hd in range(HPG):
                    split(G, hd)
            with pool.Fori(3, GROUPS) as G:
                for hd in range(HPG):
                    split(G, hd)

        @block.scalar
        def _(a):
            a.sem_inc(exp_done, 3)
            a.sem_inc(pv_copied, 1)

            def rows(G, hd, use):
                a.wait_ge(turned, use + 1)
                if not first(G):
                    a.wait_ge(rows_in[hd], 16 * G)
                nc.scalar.copy(mrows[:, hd], mp[0:PARTS * TB, 0:P // 2].bitcast(BF16))\
                    .then_inc(turned_read, 1)

            def copy_pv(G, qh):
                r = 2 * G + qh
                a.wait_ge(pv_done, (r + 1) * KT + 2)
                nc.scalar.copy(oT[:, qh], pv[:]).then_inc(pv_copied, 1)

            def group(G, u, use):
                for s in range(STEPS):
                    for j in range(HPG):
                        n = G * (STEPS * HPG) + s * HPG + j
                        a.wait_ge(x_ready, n + 1)
                        a.wait_ge(pv_done, G * STEPS + s + 1)
                        nc.scalar.activation(prob[:, (s % 2) * HPG + j], x_bank(G, u, s, j), ACT.Exp,
                                             scale=1.0 / HD ** 0.5).then_inc(exp_done, 1)
                        if j == 1 and s == 0 and not first(G):
                            copy_pv(G - 1, 1)
                        if j == 1 and s == KT:
                            copy_pv(G, 0)
                    if s in TURN_AT and exists(G + 1):
                        hd = TURN_AT[s]
                        rows(G + 1, hd, turn_of_rows(G, hd))

            for hd in range(HPG):
                rows(0, hd, hd)
            over_groups(a, group)
            copy_pv(GROUPS - 1, 1)

        @block.vector
        def _(v):
            nc.vector.memset(zero[:], 0.0).then_inc(zero_ready, 1)
            nc.vector.tensor_copy(ident16[:], ident[:]).then_inc(ident16_ready, 1)
            v.sem_inc(half_max, 3)
            v.sem_inc(turned_read, 1)

            def unit(G, u, n):
                hd, k = n // TB, n % TB
                for half in range(CPB):
                    count = CPB * (G * UNITS + n - HEADS_BEFORE * TB) + half + 1
                    v.wait_ge(s_ready, count)
                    nc.vector.tensor_reduce(mx_half[:, hd % 2, half, k:k + 1], half_bank(u, n, half), AX.X, ALU.max)\
                        .then_inc(half_max, 1)
                if k == TB - 1:
                    v.wait_ge(half_max, count + 3)
                    v.wait_ge(mx_split, G * HPG + hd + 1)
                    nc.vector.tensor_tensor(mx[:, hd % 2], mx_half[:, hd % 2, 0], mx_half[:, hd % 2, 1], ALU.max)\
                        .then_inc(row_max, 1)

            def out(G, qh):
                link = Link(v, dve_link, 2 * G + qh)
                v.wait_ge(turned, turn_of_out(G, qh) + 1)
                cols = mp[:].rearrange("p (k j c) -> p k j c", k=CT, j=HPG)
                link(nc.vector.reciprocal(rden[:], cols[:, :, :, HD]))
                nc.vector.tensor_tensor(
                    o_all[:, qh * CT:(qh + 1) * CT, ds(G, 1), :].rearrange("p k a (j d) -> p (k a) j d", j=HPG),
                    cols[:, :, :, 0:HD], rden[:].unsqueeze(3).broadcast_to([P, CT, HPG, HD]), ALU.mult)\
                    .then_inc(turned_read, 1)

            def group(G, u, use):
                for s in range(STEPS):
                    for ahead, n in units_of(G, s):
                        unit(G + ahead, (u + ahead) % 3, n)
                    if s == LAST_OUT_AT and not first(G):
                        out(G - 1, 1)
                    if s == OUT_AT:
                        out(G, 0)

            nc.vector.memset(pv[:], 0.0).then_inc(pv_zero, 1)
            over_groups(v, group)
            out(GROUPS - 1, 1)

        @block.tensor
        def _(pe):
            pe.sem_inc(pv_done, 2)
            pe.wait_ge(ident16_ready, 1)

            def unit(G, u, n, halves=range(CPB)):
                hd, k = n // TB, n % TB
                for kh in halves:
                    count = CPB * (G * UNITS + n - HEADS_BEFORE * TB) + kh + 1
                    pe.wait_ge(half_max, count)
                    nc.tensor.matmul(half_bank(u, n, kh), qs[u][0:STACK, hd, k * P:(k + 1) * P],
                                     ks[u][0:STACK, hd, kh * CH:(kh + 1) * CH], start=True, stop=True)\
                        .then_inc(s_ready, 1)

            def turn_rows(G, hd, use):
                pe.wait_ge(mx_split, G * HPG + hd + 1 + 2)
                pe.wait_ge(turned_read, use + 1)
                nc.tensor.transpose(mp[0:PARTS * TB, 0:P // 2].bitcast(BF16),
                                    mparts[:, hd % 2].rearrange("p s k -> p (s k)"), ident16[:])\
                    .then_inc(turned, 1)

            def turn_out(G, qh):
                pe.wait_ge(pv_copied, 2 * G + qh + 2)
                pe.wait_ge(turned_read, turn_of_out(G, qh) + 1)
                for k in range(CT):
                    ins = nc.tensor.transpose(mp[:, k * P:(k + 1) * P], oT[:, qh, k * P:(k + 1) * P], ident[:])
                ins.then_inc(turned, 1)

            def scores(G, u, s, j):
                qh, k = s // KT, s % KT
                n = G * (STEPS * HPG) + s * HPG + j
                if last(G) and s == 0 and j == 3:
                    pe.wait_ge(half_max, CPB * (GROUPS * UNITS - HEADS_BEFORE * TB) + 3)
                elif last(G) and s == 0:
                    pe.wait_ge(exp_done, G * (STEPS * HPG) + 3)
                elif last(G):
                    pe.wait_ge(exp_done, n)
                else:
                    pe.wait_ge(exp_done, n + 1)
                nc.tensor.matmul(x_bank(G, u, s, j), ks[u][0:ROWS, j, k * P:(k + 1) * P],
                                 qs[u][0:ROWS, j, qh * CH:(qh + 1) * CH], start=True, stop=True).then_inc(x_ready, 1)

            def values(G, u, s):
                qh, k = s // KT, s % KT
                pe.wait_ge(exp_done, G * (STEPS * HPG) + s * HPG + HPG + 3)
                if k == 0:
                    pe.wait_ge(pv_copied, 2 * G + qh + 1)
                for j in range(HPG):
                    ins = nc.tensor.matmul(pv[32 * j:32 * j + VW, :], vg[:, u, k, j, :],
                                           prob[:, (s % 2) * HPG + j], start=(k == 0), stop=(k == KT - 1))
                ins.then_inc(pv_done, 1)

            def group(G, u, use):
                for s in range(STEPS):
                    if s == 0:
                        if first(G):
                            pe.wait_ge(minus_ready, 1)
                        for hd in range(HPG):
                            pe.wait_ge(rows_in[hd], 16 * (G + 1))
                    if s == 1:
                        pe.wait_ge(v_in[u], 16 * (use + 1))
                    units = units_of(G, s)
                    for ahead, n in units:
                        if n == 0:
                            pe.wait_ge(stack_in[(u + ahead) % 3], stack_loads(u, use, ahead) * STACK_DMAS * 16)

                    def half_unit(i):
                        if i // CPB < len(units):
                            ahead, n = units[i // CPB]
                            unit(G + ahead, (u + ahead) % 3, n, [i % CPB])

                    scores(G, u, s, 0)
                    half_unit(0)
                    scores(G, u, s, 1)
                    half_unit(1)
                    if last(G):
                        scores(G, u, s, 2)
                        scores(G, u, s, 3)
                    if s > 0:
                        values(G, u, s - 1)
                    elif not first(G):
                        values(G - 1, (u + 2) % 3, STEPS - 1)
                    if not last(G):
                        scores(G, u, s, 2)
                        half_unit(2)
                        scores(G, u, s, 3)
                        half_unit(3)
                    if s == LAST_OUT_AT and not first(G):
                        turn_out(G - 1, 1)
                    if s == OUT_AT:
                        turn_out(G, 0)
                    if s in TURN_AT and exists(G + 1):
                        turn_rows(G + 1, TURN_AT[s], turn_of_rows(G, TURN_AT[s]))

            for hd in range(HPG):
                turn_rows(0, hd, hd)
            pe.wait_ge(pv_zero, 1)
            over_groups(pe, group)
            values(GROUPS - 1, (GROUPS - 1) % 3, STEPS - 1)
            turn_out(GROUPS - 1, 1)


def project_out(nc, t, xg, o_all, xin, wo, bo, ident):
    with ExitStack() as ctx:
        sb = lambda name, shape, dt=F32: ctx.enter_context(nc.sbuf_tensor(name, shape, dt))
        sem = lambda name: ctx.enter_context(nc.semaphore(name))
        SLOTS = 4
        wo2 = [sb(f"wo2_{i}", [P, KC, D], F32R) for i in range(2)]
        oT = [sb(f"oT3_{i}", [P, 2, KC, CH], F32R) for i in range(2)]
        gate = sb("gate", [P, 2, CT, D])
        res = sb("res", [P, SLOTS, CT, D])
        tp = ctx.enter_context(nc.psum_tensor("tp", [P, 2, KC, CH], F32))
        spj = ctx.enter_context(nc.psum_tensor("spj", [P, 2, CT, D], F32))
        wo_high, wo_low = sem("wo_high"), sem("wo_low")
        t_done, oT_high, oT_low = sem("t_done3"), sem("oT_high"), sem("oT_low")
        s_ready, s_biased = sem("s_ready3"), sem("s_biased")
        gate_ready, gated, res_ready = sem("gate_ready"), sem("gated"), sem("res_ready")
        last_gated = sem("last_gated")
        stored = [sem(f"stored{i}") for i in range(SLOTS)]
        block = ctx.enter_context(nc.Block())
        ov = t["out"].rearrange("(c k p) d -> c p k d", p=P, k=CT)
        CHUNKS = N // CH

        @block.sync
        def _(sp):
            for c in range(CHUNKS):
                sp.wait_ge(res_ready, c + 1)
                sp.dma_start(ov[c], res[:, c % SLOTS]).then_inc(stored[c % SLOTS], 16)
            for s in stored:
                sp.wait_ge(s, 16 * CHUNKS // SLOTS)

        @block.gpsimd
        def _(pool):
            for c in range(CHUNKS - 1):
                pool.wait_ge(s_biased, c + 1)
                pool.wait_ge(gate_ready, c + 1)
                nc.gpsimd.tensor_tensor(res[:, c % SLOTS], res[:, c % SLOTS], gate[:, c % 2], ALU.mult)\
                    .then_inc(gated, 1)

        @block.scalar
        def _(a):
            def high(c):
                a.wait_ge(t_done, c + 1)
                if c >= 2:
                    a.wait_ge(s_ready, c - 1)
                nc.scalar.copy(oT[0][:, c % 2], tp[:, c % 2]).then_inc(oT_high, 1)

            nc.scalar.copy(wo2[0][:], wo[:]).then_inc(wo_high, 1)
            high(0)
            for c in range(CHUNKS):
                if c >= 2:
                    a.wait_ge(gated, c - 1)
                nc.scalar.activation(gate[:, c % 2], xg[:, c * CT:(c + 1) * CT, :], ACT.Silu).then_inc(gate_ready, 1)
                if c + 1 < CHUNKS:
                    high(c + 1)

        @block.vector
        def _(v):
            def finish(c):
                if c < CHUNKS - 1:
                    v.wait_ge(gated, c + 1)
                else:
                    v.wait_ge(gate_ready, c + 1)
                    v.wait_ge(s_biased, c + 1)
                    nc.vector.tensor_tensor(res[:, c % SLOTS], res[:, c % SLOTS], gate[:, c % 2], ALU.mult)\
                        .then_inc(last_gated, 1)
                    v.wait_ge(last_gated, 1)
                nc.vector.tensor_tensor(res[:, c % SLOTS], res[:, c % SLOTS], xin[:, c * CT:(c + 1) * CT, :], ALU.add)\
                    .then_inc(res_ready, 1)

            def low(c):
                v.wait_ge(oT_high, c + 1)
                nc.vector.tensor_tensor(oT[1][:, c % 2], tp[:, c % 2], oT[0][:, c % 2].bitcast(F32), ALU.subtract)\
                    .then_inc(oT_low, 1)

            v.wait_ge(wo_high, 1)
            nc.vector.tensor_tensor(wo2[1][:], wo[:], wo2[0][:].bitcast(F32), ALU.subtract).then_inc(wo_low, 1)
            low(0)
            for c in range(CHUNKS):
                if c + 1 < CHUNKS:
                    low(c + 1)
                v.wait_ge(s_ready, c + 1)
                if c >= SLOTS:
                    v.wait_ge(stored[c % SLOTS], 16 * (c // SLOTS))
                nc.vector.tensor_tensor(res[:, c % SLOTS], spj[:, c % 2],
                                        bo[:].unsqueeze(1).broadcast_to([P, CT, D]), ALU.add)\
                    .then_inc(s_biased, 1)
                if c >= 1:
                    finish(c - 1)
            finish(CHUNKS - 1)

        @block.tensor
        def _(pe):
            channels = o_all[:].rearrange("p k (b g) w -> p k b (g w)", b=NB)

            def turn(c):
                if c >= 2:
                    pe.wait_ge(oT_low, c - 1)
                b, first = c // CPB, c % CPB * CT
                for k in range(CT):
                    for h in range(KC):
                        ins = nc.tensor.transpose(tp[:, c % 2, h, k * P:(k + 1) * P],
                                                  channels[:, first + k, b, h * P:(h + 1) * P], ident[:])
                ins.then_inc(t_done, 1)

            turn(0)
            pe.wait_ge(wo_low, 1)
            for c in range(CHUNKS):
                if c + 1 < CHUNKS:
                    turn(c + 1)
                pe.wait_ge(oT_low, c + 1)
                if c >= 2:
                    pe.wait_ge(s_biased, c - 1)
                for k in range(CT):
                    products = [(h, wp, op) for h in range(KC) for wp, op in PASSES]
                    for m, (h, wp, op) in enumerate(products):
                        ins = nc.tensor.matmul(spj[:, c % 2, k], oT[op][:, c % 2, h, k * P:(k + 1) * P],
                                               wo2[wp][:, h, :], start=(m == 0), stop=(m == len(products) - 1))
                ins.then_inc(s_ready, 1)


def build(nc, t):
    with ExitStack() as ctx:
        xg = ctx.enter_context(nc.sbuf_tensor("xg", [P, TILES, D], F32))
        ident = ctx.enter_context(nc.sbuf_tensor("ident", [P, P], F32))
        scr = {
            "qk": nc.dram_tensor("qk_parts", [CPB * GROUPS, 2, PARTS, HPG * HD, CH], BF16).ap(),
            "v": nc.dram_tensor("v_ones", [GROUPS, P, KT * HPG * VW], F32).ap(),
        }
        stack0 = ctx.enter_context(nc.sbuf_tensor("stack0", [P, 2 * TB * D], F32))
        stack1 = ctx.enter_context(nc.sbuf_tensor("stack1", [P, max(HPG * T, VST + 4 * CH)], F32))
        mx0 = ctx.enter_context(nc.sbuf_tensor("mx0", [P, HEADS_BEFORE, TB], F32))
        project_and_ffn(nc, t, scr, xg, stack0, stack1, mx0, ident)
        o_all = ctx.enter_context(nc.sbuf_tensor("o_all", [P, TB, GROUPS, HPG * HD], F32))
        xin = ctx.enter_context(nc.sbuf_tensor("xin", [P, TILES, D], F32))
        wo = ctx.enter_context(nc.sbuf_tensor("wo_sb", [P, KC, D], F32))
        bo = ctx.enter_context(nc.sbuf_tensor("bo_sb", [P, D], F32))
        attention(nc, t, scr, stack0, stack1, mx0, o_all, xin, wo, bo, ident)
        project_out(nc, t, xg, o_all, xin, wo, bo, ident)


def kernel(**inputs):
    import numpy as np
    import concourse.bacc as bacc
    from concourse.bass_utils import run_bass_kernel_spmd

    a = {k[3:]: np.asarray(v) for k, v in inputs.items()}

    def by_contraction(w):
        return np.ascontiguousarray(w.T.reshape(KC, P, -1).transpose(1, 0, 2))

    def by_dim(w):
        return w.reshape(2 * GPB, HPG, HD, -1).transpose(0, 2, 1, 3).reshape(w.shape)

    def experts(w, shared):
        w = np.concatenate([shared.reshape(-1, I, D), w])
        return w.transpose(0, 2, 1).reshape(-1, KC, P, I).transpose(0, 2, 1, 3).reshape(-1, P, KC * I)

    wd = np.concatenate([a["ffn_Ws_d"].T.reshape(-1, I, D), a["ffn_Wd"].transpose(0, 2, 1)])
    arrays = {
        "x": a["attn_x"].reshape(N, D),
        "wqk": by_contraction(by_dim(a["attn_W_qkv"][0:2 * D])),
        "wvg": by_contraction(np.concatenate([a["attn_W_qkv"][2 * D:], a["ffn_gate_w"]])),
        "bqk": np.ascontiguousarray(by_dim(a["attn_b_qkv"][0:2 * D]).reshape(4, P).T),
        "bv": a["attn_b_qkv"][2 * D:].reshape(1, D),
        "gbias": a["ffn_gate_bias"].reshape(1, E),
        "we": np.concatenate([experts(a["ffn_Wg"], a["ffn_Ws_g"]), experts(a["ffn_Wu"], a["ffn_Ws_u"]), wd], 2),
        "wo": by_contraction(a["attn_W_o"]),
        "bo": a["attn_b_o"].reshape(1, D),
    }
    nc = bacc.Bacc("TRN2", target_bir_lowering=False, num_devices=1)
    t = {k: nc.dram_tensor(f"{k}_dram", v.shape, F32, kind="ExternalInput").ap() for k, v in arrays.items()}
    t["out"] = nc.dram_tensor("out_dram", (N, D), F32, kind="ExternalOutput").ap()
    build(nc, t)
    r = run_bass_kernel_spmd(nc, [{f"{k}_dram": v for k, v in arrays.items()}], core_ids=[0])
    return r.results[0]["out_dram"].reshape(NB, T, D)
```
